# Optimizing a Trainium2 kernel written in Bass

```python
import numpy as np
import jax
import jax.numpy as jnp

def _softmax(x, axis=-1):
    return jax.nn.softmax(x, axis=axis)

def _gelu(x):
    return jax.nn.gelu(x, approximate=True)

def _silu(x):
    return jax.nn.silu(x)

def _sigmoid(x):
    return jax.nn.sigmoid(x)

def _layernorm(x, axis=-1, eps=1e-05):
    m = jnp.mean(x, axis=axis, keepdims=True)
    v = jnp.var(x, axis=axis, keepdims=True)
    return (x - m) / jnp.sqrt(v + eps)

def _scatter_add(tgt, idx, src, axis=0):
    return tgt.at[idx].add(src)

def _segment_sum(src, seg, n):
    return jax.ops.segment_sum(src, seg, n)
kernel_name = 'mk_gnn_resnorm_d1_gnn_r64_16dd03'

def setup_inputs(seed: int=0):
    np.random.seed(seed)
    _w = jnp.asarray

    def _rec_inputs():
        import jax
        import jax.numpy as jnp
        _gk = jax.random.key(seed)
        x = -0.0001006 + 1 * jax.random.normal(jax.random.fold_in(_gk, 1), (100000, 96), jnp.float32)
        src = jax.random.randint(jax.random.fold_in(_gk, 2), (25000,), 0, 100000, jnp.int32)
        dst = jax.random.randint(jax.random.fold_in(_gk, 3), (25000,), 0, 100000, jnp.int32)
        _o = jnp.argsort(dst, stable=True)
        src = src[_o]
        dst = dst[_o]
        edge_attr_32 = 0.000196303 + 1.00016 * jax.random.normal(jax.random.fold_in(_gk, 11), (25000, 32), jnp.float32)
        return (x, src, dst, edge_attr_32)
    x, src, dst, edge_attr_32 = _rec_inputs()

    def _L0_gnn_setup():
        import jax, jax.numpy as jnp
        import numpy as np
        N, E = (50000, 12500)
        DIN = DOUT = 96
        DE = 32

        def _egnn_conv(x, src, dst, edge_attr, W_msg, W_edge, W_root, b):
            msg = x[src] @ W_msg + edge_attr @ W_edge
            agg = jax.ops.segment_max(msg, dst, num_segments=x.shape[0])
            agg = jnp.where(jnp.isneginf(agg), 0.0, agg)
            return agg + x @ W_root + b
        key = jax.random.key(seed)
        ks = jax.random.split(key, 10)
        rn = lambda k, sh, sc: jax.random.normal(k, sh, jnp.float32) * sc
        return {'X': rn(ks[0], (N, DIN), 1.0), 'edge_index': jax.random.randint(ks[1], (2, E), 0, N, jnp.int32), 'edge_attr': rn(ks[2], (E, DE), 1.0), 'W1_msg': rn(ks[3], (DIN, DOUT), DIN ** (-0.5)), 'W1_edge': rn(ks[4], (DE, DOUT), DE ** (-0.5)), 'W1_root': rn(ks[5], (DIN, DOUT), DIN ** (-0.5)), 'b1': jnp.zeros((DOUT,), jnp.float32), 'W2_msg': rn(ks[6], (DOUT, DOUT), DOUT ** (-0.5)), 'W2_edge': rn(ks[7], (DE, DOUT), DE ** (-0.5)), 'W2_root': rn(ks[8], (DOUT, DOUT), DOUT ** (-0.5)), 'b2': jnp.zeros((DOUT,), jnp.float32)}
    _L0_gnn_all = _L0_gnn_setup()
    _L0_gnn_in = {k: v for k, v in _L0_gnn_all.items() if k in ('W1_msg', 'W1_edge', 'W1_root', 'b1', 'W2_msg', 'W2_edge', 'W2_root', 'b2')}
    del _L0_gnn_all
    return {'x': x, 'src': src, 'dst': dst, 'edge_attr_32': edge_attr_32, 'L0_gnn_W1_msg': _L0_gnn_in['W1_msg'], 'L0_gnn_W1_edge': _L0_gnn_in['W1_edge'], 'L0_gnn_W1_root': _L0_gnn_in['W1_root'], 'L0_gnn_b1': _L0_gnn_in['b1'], 'L0_gnn_W2_msg': _L0_gnn_in['W2_msg'], 'L0_gnn_W2_edge': _L0_gnn_in['W2_edge'], 'L0_gnn_W2_root': _L0_gnn_in['W2_root'], 'L0_gnn_b2': _L0_gnn_in['b2']}

def reference(x, src, dst, edge_attr_32, L0_gnn_W1_msg, L0_gnn_W1_edge, L0_gnn_W1_root, L0_gnn_b1, L0_gnn_W2_msg, L0_gnn_W2_edge, L0_gnn_W2_root, L0_gnn_b2):
    import jax
    import jax.numpy as jnp

    def _L0_gnn_ref(X, edge_index, edge_attr, W1_msg, W1_edge, W1_root, b1, W2_msg, W2_edge, W2_root, b2):
        import jax, jax.numpy as jnp
        import numpy as np
        N, E = (50000, 12500)
        DIN = DOUT = 96
        DE = 32

        def _egnn_conv(x, src, dst, edge_attr, W_msg, W_edge, W_root, b):
            msg = x[src] @ W_msg + edge_attr @ W_edge
            agg = jax.ops.segment_max(msg, dst, num_segments=x.shape[0])
            agg = jnp.where(jnp.isneginf(agg), 0.0, agg)
            return agg + x @ W_root + b
        src, dst = (edge_index[0], edge_index[1])
        c1 = jax.nn.leaky_relu(_egnn_conv(X, src, dst, edge_attr, W1_msg, W1_edge, W1_root, b1))
        c2 = jax.nn.leaky_relu(_egnn_conv(c1, src, dst, edge_attr, W2_msg, W2_edge, W2_root, b2))
        return c2
    edge_index = jnp.stack([src, dst])
    x = _layernorm(x + _L0_gnn_ref(x, edge_index, edge_attr_32, L0_gnn_W1_msg, L0_gnn_W1_edge, L0_gnn_W1_root, L0_gnn_b1, L0_gnn_W2_msg, L0_gnn_W2_edge, L0_gnn_W2_root, L0_gnn_b2), axis=-1)
    return x

_drawn_inputs = setup_inputs


def setup_inputs(seed=0):
    import zlib

    import numpy as np

    out = dict(_drawn_inputs(seed))
    spreads = {'L0_gnn_b1': (0.0, 0.1), 'L0_gnn_b2': (0.0, 0.1)}
    factors = {}
    for name, (base, spread) in spreads.items():
        noise = np.random.default_rng([zlib.crc32(name.encode()), seed]).standard_normal(out[name].shape)
        drawn = base * np.exp(spread * noise) if base else spread * noise
        out[name] = jnp.asarray(drawn.astype(out[name].dtype))
    for name, factor in factors.items():
        out[name] = (out[name] * factor).astype(out[name].dtype)
    return out
```

```python
import concourse.bass as bass
from concourse import mybir
from contextlib import ExitStack

P = 128
N, D = 100000, 96
E, DE = 25000, 32
TPC = 4
CH = TPC * P
NCH = -(-E // CH)
EP = NCH * CH
NT = NCH * TPC
NB = -(-N // CH)
TAIL_P = (N - (NB - 1) * CH) // TPC
R = 4
FAR = 1 << 20
FMAX = 3.4028234663852886e38
EPS = 1e-5
SLOPE = 0.01
ZCOL = 3000
assert N * D % (P * ZCOL) == 0 and NB == 4 * NCH and NCH % R == 1


class Step:

    def __init__(self, q, a, b):
        self.q, self.a, self.b = q, a, b

    @property
    def at(self):
        return self.q * self.a + self.b

    def before(self, k):
        return Step(self.q, self.a, self.b - k)

    def slot(self, n):
        assert self.a % n == 0
        return self.b % n

    def turn(self, n):
        assert self.a % n == 0
        return self.q * (self.a // n) + self.b // n

    def reached(self, k):
        return self.a * (self.q if isinstance(self.q, int) else 1) + self.b >= k


def each_chunk(eng, step):
    for s in range(R):
        step(0, s)
    with eng.Fori(1, NCH // R) as q:
        for s in range(R):
            step(q, s)
    step(NCH // R, 0, last=True)


def chunk(q, s):
    return Step(q, R, s)


def block_a(q, s):
    return Step(q, R, s)


def block_s(q, s):
    return Step(q, R, NCH + s)


def block_b(q, s, t):
    return Step(q, 2 * R, 2 * NCH + 2 * s + t)


LAST_CHUNK = Step(NCH // R, R, 0)
LAST_BLOCK = Step(0, R, NB - 1)


def gnn_kernel(nc, x, xt, src, dst, dst_next, dst_row, dst_prev, eat,
               w1m, w1e, w1r, b1, w2m, w2e, w2r, b2, out):
    f32 = mybir.dt.float32
    i32 = mybir.dt.int32
    ALU = mybir.AluOpType
    ACT = mybir.ActivationFunctionType
    ds = bass.ds

    table = nc.dram_tensor("agg1_table", (N, D), f32, kind="Internal").ap()
    mask_row = nc.dram_tensor("mask_row", (P, NT), f32, kind="Internal").ap()
    root_keep = nc.dram_tensor("root_keep", (NCH, D, CH), f32, kind="Internal").ap()
    max_keep = nc.dram_tensor("max_keep", (NCH, D, CH), f32, kind="Internal").ap()
    table_z = table.rearrange("n d -> (n d)").rearrange("(k p c) -> k p c", p=P, c=ZCOL)
    mask_c = mask_row.rearrange("p t -> (p t)").rearrange("(c o e) -> c o e", o=1, e=CH)
    out_b = out[0:(NB - 1) * CH, :].rearrange("(b p j) d -> b p (j d)", p=P, j=TPC)
    out_tail = out[(NB - 1) * CH:N, :].rearrange("(p j) d -> p (j d)", j=TPC)

    ctx = ExitStack()
    with ctx:
        def sb(name, shape, dt=f32):
            return ctx.enter_context(nc.sbuf_tensor(name, shape, dt))

        def pb(name, shape):
            return ctx.enter_context(nc.psum_tensor(name, shape, f32))

        def sem(name):
            return ctx.enter_context(nc.semaphore(name))

        def sems(name, n):
            return [sem(f"{name}{i}") for i in range(n)]

        ident = sb("ident", [P, P])
        wm1 = sb("wm1", [P, D])
        wm2 = sb("wm2", [P, D])
        wr1 = sb("wr1", [D + 1, D])
        wr2 = sb("wr2", [D + 1, D])
        b1c = sb("b1c", [D, 1])
        b2c = sb("b2c", [D, 1])
        epsc = sb("epsc", [P, 1])
        zero = sb("zero", [P, ZCOL])
        src_i = sb("src_i", [P, NT], i32)
        dst_i = sb("dst_i", [P, NT], i32)
        dst_n = sb("dst_n", [P, NT], i32)
        own_i = sb("own_i", [P, NT], i32)
        end_i = sb("end_i", [P, NT], i32)
        eq_c = sb("eq_c", [P, NT])
        row_d = sb("row_d", [P, NT], i32)
        row_p = sb("row_p", [P, NT], i32)
        row_m = sb("row_m", [P, NT])
        now_src = sb("now_src", [P, R, TPC], i32)
        now_own = sb("now_own", [P, R, TPC], i32)
        now_end = sb("now_end", [P, R, TPC], i32)
        g_src = sb("g_src", [P, R, TPC * D])
        g_dst = sb("g_dst", [P, R, TPC * D])
        xe = sb("xe", [P, R, CH])
        mask = sb("mask", [D, R, CH])
        mx1 = sb("mx1", [D, R, CH])
        rt1 = sb("rt1", [D, R, CH])
        mx2 = sb("mx2", [D, 2, CH])
        xd = sb("xd", [D, 2, CH])
        c1d = sb("c1d", [D, 2, CH])
        yd = sb("yd", [D, 2, CH])
        nat = sb("nat", [P, NT * D])
        stage = sb("stage", [P, 2, TPC * D])
        xtb = sb("xtb", [D + 1, R, CH])
        c1t = sb("c1t", [D + 1, 2, CH])
        c2t = sb("c2t", [D, 2, CH])
        ob = sb("ob", [P, R, TPC * D])
        stat = sb("stat", [P, 4, TPC, 6])
        mv = sb("mv", [P, 4, TPC, 2])
        std = sb("std", [P, 4, TPC])
        rstd = sb("rstd", [P, 4, TPC])
        shift = sb("shift", [P, 2, TPC])
        idle = sb("idle", [1, 1])

        ps_t = pb("ps_t", [P, CH])
        ps_m = pb("ps_m", [P, CH])
        ps_r = pb("ps_r", [P, CH])
        ps_n = pb("ps_n", [P, CH])
        ps_r2 = pb("ps_r2", [P, CH])
        ps_1 = pb("ps_1", [P, CH])
        ps_2 = pb("ps_2", [P, CH])
        ps_y = pb("ps_y", [P, CH])

        s_const = sem("s_const")
        s_index = sem("s_index")
        s_ident0 = sem("s_ident0")
        s_ident = sem("s_ident")
        s_zero = sem("s_zero")
        s_epsc = sem("s_epsc")
        s_ones = sem("s_ones")
        s_prep = sem("s_prep")
        s_mask_w = sem("s_mask_w")
        s_cleared = sem("s_cleared")
        l_src = sems("l_src", R)
        l_dst = sems("l_dst", R)
        l_ea = sems("l_ea", R)
        l_mask = sems("l_mask", R)
        l_xt = sems("l_xt", R)
        l_rt = sems("l_rt", R)
        l_mx = sems("l_mx", R)
        k_rt = sems("k_rt", R)
        k_mx = sems("k_mx", R)
        o_st = sems("o_st", R)
        sc = sems("sc", 2)
        s_now = sem("s_now")
        a_t = sem("a_t")
        a_xe = sem("a_xe")
        a_m = sem("a_m")
        a_scan = sem("a_scan")
        a_r = sem("a_r")
        a_rc = sem("a_rc")
        a_n = sem("a_n")
        a_nc = sem("a_nc")
        s_stage = sem("s_stage")
        t_own = sem("t_own")
        t_agg = sem("t_agg")
        v_agg = sem("v_agg")
        c_src = sem("c_src")
        c_xd = sem("c_xd")
        p_m = sem("p_m")
        v_scan = sem("v_scan")
        p_r1 = sem("p_r1")
        v_1 = sem("v_1")
        c_1 = sem("c_1")
        p_r2 = sem("p_r2")
        v_2 = sem("v_2")
        c_2 = sem("c_2")
        v_y = sem("v_y")
        p_n = sem("p_n")
        c_n = sem("c_n")
        d_1 = sem("d_1")
        d_e1 = sem("d_e1")
        d_c1 = sem("d_c1")
        d_2 = sem("d_2")
        d_e2 = sem("d_e2")
        d_c2 = sem("d_c2")
        d_y = sem("d_y")
        d_n = sem("d_n")
        ln = [dict(stats=sem(f"ln_stats{k}"), mv=sem(f"ln_mv{k}"), std=sem(f"ln_std{k}"),
                   rstd=sem(f"ln_rstd{k}"), shift=sem(f"ln_shift{k}"), done=sem(f"ln_done{k}")) for k in "de"]
        DENSE, EDGE = 0, 1

        block = ctx.enter_context(nc.Block())

        def cols(j):
            return slice(j * P, (j + 1) * P)

        def row(j):
            return slice(j * D, (j + 1) * D)

        @block.gpsimd
        def _(pool):
            nc.gpsimd.memset(ident[:, :], 0.0).then_inc(s_ident0, 1)
            pool.wait_ge(s_ident0, 1)
            nc.gpsimd.affine_select(out=ident[:, :], in_=ident[:, :], compare_op=ALU.not_equal,
                                    fill=1.0, base=0, pattern=[[-1, P]],
                                    channel_multiplier=1).then_inc(s_ident, 1)

            def stage_index(now, index, c):
                return nc.gpsimd.tensor_copy(now[:, c.slot(R), :], index[:, ds(c.at * TPC, TPC)])

            def gather(rows, where, now, c, e, landed):
                for r in range(TPC):
                    nc.gpsimd.indirect_dma_start(
                        out=where[:, e.slot(R), row(r)], out_offset=None, in_=rows,
                        in_offset=bass.IndirectOffsetOnAxis(ap=now[:, c.slot(R), r:r + 1], axis=0),
                    ).then_inc(landed[e.slot(R)], 16)

            def scatter(rows, c, k):
                for r in range(TPC):
                    nc.gpsimd.indirect_dma_start(
                        out=rows,
                        out_offset=bass.IndirectOffsetOnAxis(ap=now_end[:, c.slot(R), r:r + 1], axis=0),
                        in_=stage[:, k, row(r)], in_offset=None, bounds_check=N - 1,
                        oob_is_err=False).then_inc(sc[k], 16)

            pool.wait_ge(s_index, 5 * 16)
            pool.wait_ge(s_prep, 6)
            stage_index(now_src, src_i, chunk(0, 0)).then_inc(s_now, 1)

            def gather_a(q, s, last=False):
                c = chunk(q, s)
                if c.reached(R - 1):
                    pool.wait_ge(l_src[c.before(R - 1).slot(R)], 64 * c.before(R - 1).turn(R) + 64)
                if c.reached(R):
                    pool.wait_ge(a_t, c.before(R - 1).at)
                pool.wait_ge(s_now, c.at + 1)
                if not last:
                    stage_index(now_src, src_i, chunk(q, s + 1)).then_inc(s_now, 1)
                gather(x, g_src, now_src, c, c, l_src)

            each_chunk(pool, gather_a)
            pool.wait_ge(s_cleared, 16 * (N * D // (P * ZCOL)))

            def scatter_all(rows, base_stage, base_now, staged):
                stage_index(now_end, end_i, chunk(0, 0)).then_inc(s_now, 1)

                def go(q, s, last=False):
                    c = chunk(q, s)
                    e = Step(q, R, base_stage + s)
                    k = e.slot(2)
                    if e.reached(R - 1):
                        f = e.before(R - 1)
                        pool.wait_ge(sc[f.slot(2)], 64 * f.turn(2) + 64)
                    pool.wait_ge(staged, c.at + 1)
                    pool.wait_ge(s_now, c.at + base_now + 1)
                    if not last:
                        stage_index(now_end, end_i, chunk(q, s + 1)).then_inc(s_now, 1)
                    scatter(rows, c, k)

                each_chunk(pool, go)

            scatter_all(table, 0, NCH, s_stage)
            for k in range(2):
                pool.wait_ge(sc[k], 64 * ((NCH + 1 - k) // 2))
            for k in range(R):
                pool.wait_ge(l_src[k], 64 * ((NCH + R - 1 - k) // R))

            def stage_both(c):
                stage_index(now_src, src_i, c)
                stage_index(now_own, own_i, c).then_inc(s_now, 1)

            stage_both(chunk(0, 0))

            def gather_b(q, s, last=False):
                c = chunk(q, s)
                e = Step(q, R, NCH + s)
                if c.reached(R - 1):
                    f, g = e.before(R - 1), c.before(R - 1)
                    pool.wait_ge(l_src[f.slot(R)], 64 * f.turn(R) + 64)
                    pool.wait_ge(l_dst[g.slot(R)], 64 * g.turn(R) + 64)
                if c.reached(R):
                    pool.wait_ge(t_own, c.before(R - 1).at)
                    pool.wait_ge(t_agg, c.before(R - 1).at)
                pool.wait_ge(s_now, c.at + 2 * NCH + 1)
                if not last:
                    stage_both(chunk(q, s + 1))
                gather(x, g_dst, now_own, c, c, l_dst)
                gather(table, g_src, now_src, c, e, l_src)

            pool.wait_ge(a_t, NCH)
            each_chunk(pool, gather_b)
            for k in range(R):
                pool.wait_ge(o_st[k], 16 * ((NB + R - 1 - k) // R))
            scatter_all(out, NCH, 3 * NCH, ln[EDGE]["done"])
            for k in range(2):
                pool.wait_ge(sc[k], 64 * ((2 * NCH + 1 - k) // 2))

        @block.sync
        def _(sp):
            sp.dma_start(src_i[:, :], src).then_inc(s_index, 16)
            sp.dma_start(dst_i[:, :], dst).then_inc(s_index, 16)
            sp.dma_start(dst_n[:, :], dst_next).then_inc(s_index, 16)
            sp.dma_start(row_d[:, :], dst_row).then_inc(s_index, 16)
            sp.dma_start(row_p[:, :], dst_prev).then_inc(s_index, 16)
            for to, of in ((wm1[0:D, :], w1m), (wm1[D:P, :], w1e), (wr1[0:D, :], w1r), (b1c[:, :], b1),
                           (wm2[0:D, :], w2m), (wm2[D:P, :], w2e), (wr2[0:D, :], w2r), (b2c[:, :], b2),
                           (wr1[D:D + 1, :], b1.rearrange("d o -> o d")),
                           (wr2[D:D + 1, :], b2.rearrange("d o -> o d"))):
                sp.dma_start(to, of).then_inc(s_const, 16)
            sp.wait_ge(s_prep, 6)
            sp.dma_start(mask_row, row_m[:, :]).then_inc(s_mask_w, 16)
            sp.wait_ge(s_mask_w, 16)

            def load_block(d):
                if d.reached(R):
                    sp.wait_ge(d_y, d.before(R - 1).at)
                sp.dma_start(xtb[0:D, d.slot(R), :], xt[ds(d.at, 1), :, :].rearrange("o d e -> d (o e)"))\
                  .then_inc(l_xt[d.slot(R)], 16)

            def store_block(d):
                if d.reached(0):
                    sp.wait_ge(ln[DENSE]["done"], d.at + 1)
                    sp.dma_start(out_b[ds(d.at, 1), :, :].rearrange("o p f -> p (o f)"),
                                 ob[:, d.slot(R), :]).then_inc(o_st[d.slot(R)], 16)

            def load_edges(c, e, used, scanned):
                k = e.slot(R)
                if c.reached(R):
                    sp.wait_ge(used, c.before(R - 1).at)
                    sp.wait_ge(scanned, c.before(R - 1).at)
                sp.dma_start(xe[D:P, k, :], eat[ds(c.at, 1), :, :].rearrange("o d e -> d (o e)"))\
                  .then_inc(l_ea[k], 16)
                sp.dma_start(mask[:, k, :],
                             mask_c[ds(c.at, 1), :, :].rearrange("c o e -> (c o) e").to_broadcast([D, CH]))\
                  .then_inc(l_mask[k], 16)

            def keep(c):
                if c.reached(0):
                    k = c.slot(R)
                    sp.wait_ge(a_scan, c.at + 1)
                    sp.dma_start(max_keep[ds(c.at, 1), :, :].rearrange("o d e -> d (o e)"), mx1[:, k, :])\
                      .then_inc(k_mx[k], 16)
                    sp.wait_ge(a_rc, c.at + 1)
                    sp.dma_start(root_keep[ds(c.at, 1), :, :].rearrange("o d e -> d (o e)"), rt1[:, k, :])\
                      .then_inc(k_rt[k], 16)

            def step_a(q, s, last=False):
                c = chunk(q, s)
                load_edges(c, c, a_r, a_scan)
                load_block(block_a(q, s))
                keep(c.before(2))
                store_block(block_a(q, s).before(R))

            each_chunk(sp, step_a)
            keep(LAST_CHUNK.before(1))
            keep(LAST_CHUNK)

            def step_s(q, s, last=False):
                d = block_s(q, s)
                load_block(d)
                store_block(d.before(R))

            each_chunk(sp, step_s)
            for k in range(R):
                sp.wait_ge(k_mx[k], 16 * ((NCH + R - 1 - k) // R))
                sp.wait_ge(k_rt[k], 16 * ((NCH + R - 1 - k) // R))
            sp.wait_ge(a_r, NCH)
            sp.wait_ge(a_n, NCH)

            def step_b(q, s, last=False):
                c = chunk(q, s)
                k = c.slot(R)
                e = Step(q, R, NCH + s)
                if c.reached(R):
                    sp.wait_ge(c_src, c.before(R - 1).at)
                sp.dma_start(rt1[:, k, :], root_keep[ds(c.at, 1), :, :].rearrange("o d e -> d (o e)"))\
                  .then_inc(l_rt[k], 16)
                if c.reached(R):
                    sp.wait_ge(c_1, c.before(R - 1).at)
                sp.dma_start(mx1[:, k, :], max_keep[ds(c.at, 1), :, :].rearrange("o d e -> d (o e)"))\
                  .then_inc(l_mx[k], 16)
                load_block(block_b(q, s, 0))
                load_edges(c, e, p_m, v_scan)
                store_block(block_b(q, s, 0).before(R))
                load_block(block_b(q, s, 1))
                store_block(block_b(q, s, 1).before(R))

            each_chunk(sp, step_b)
            for i in range(R - 1, 0, -1):
                store_block(LAST_BLOCK.before(i))
            sp.wait_ge(ln[DENSE]["done"], NB)
            sp.dma_start(out_tail, ob[0:TAIL_P, LAST_BLOCK.slot(R), :])\
              .then_inc(o_st[LAST_BLOCK.slot(R)], 16)
            for k in range(R):
                sp.wait_ge(o_st[k], 16 * ((NB + R - 1 - k) // R))

        @block.tensor
        def _(pe):
            pe.wait_ge(s_ident, 1)
            pe.wait_ge(s_const, 10 * 16)
            pe.wait_ge(s_ones, 2)

            def forward(ps, rows, done):
                for r in range(TPC):
                    last = nc.tensor.transpose(ps[0:D, cols(r)], rows[:, row(r)], ident[:, :])
                last.then_inc(done, 1)

            def back(ps, t, done):
                for r in range(TPC):
                    last = nc.tensor.transpose(ps[:, row(r)], t[:, cols(r)], ident[0:D, 0:D])
                last.then_inc(done, 1)

            def product(ps, w, t, done):
                nc.tensor.matmul(ps[0:D, :], w, t, start=True, stop=True).then_inc(done, 1)

            def dense_1(d):
                pe.wait_ge(l_xt[d.slot(R)], 16 * d.turn(R) + 16)
                if d.reached(1):
                    pe.wait_ge(d_e1, d.at)
                product(ps_1, wr1[:, :], xtb[:, d.slot(R), :], d_1)

            def dense_2(d):
                pe.wait_ge(d_c1, d.at + 1)
                if d.reached(1):
                    pe.wait_ge(d_e2, d.at)
                product(ps_2, wr2[:, :], c1t[:, d.slot(2), :], d_2)

            def dense_back(d):
                if d.reached(0):
                    pe.wait_ge(d_y, d.at + 1)
                    if d.reached(1):
                        pe.wait_ge(ln[DENSE]["done"], d.at)
                    back(ps_y, c2t[:, d.slot(2), :], d_n)

            def step_a(q, s, last=False):
                c, d = chunk(q, s), block_a(q, s)
                k = c.slot(R)
                pe.wait_ge(l_src[k], 64 * c.turn(R) + 64)
                if c.reached(1):
                    pe.wait_ge(a_xe, c.at)
                forward(ps_t, g_src[:, k, :], a_t)
                dense_1(d)
                dense_back(d.before(1))
                pe.wait_ge(a_xe, c.at + 1)
                pe.wait_ge(l_ea[k], 16 * c.turn(R) + 16)
                if c.reached(1):
                    pe.wait_ge(a_scan, c.at)
                product(ps_m, wm1[:, :], xe[:, k, :], a_m)
                if c.reached(1):
                    pe.wait_ge(a_rc, c.at)
                product(ps_r, wr1[0:D, :], xe[0:D, k, :], a_r)
                dense_2(d)
                pe.wait_ge(a_scan, c.at + 1)
                if c.reached(1):
                    pe.wait_ge(a_nc, c.at)
                back(ps_n, mx1[:, k, :], a_n)

            each_chunk(pe, step_a)

            def step_s(q, s, last=False):
                d = block_s(q, s)
                dense_1(d)
                dense_back(d.before(1))
                dense_2(d)

            each_chunk(pe, step_s)
            pe.wait_ge(a_xe, NCH)
            pe.wait_ge(a_rc, NCH)
            pe.wait_ge(a_nc, NCH)

            def back_b(c):
                if c.reached(0):
                    pe.wait_ge(v_y, c.at + 1)
                    if c.reached(1):
                        pe.wait_ge(c_n, c.at)
                    back(ps_n, yd[:, c.slot(2), :], p_n)

            def step_b(q, s, last=False):
                c, d0, d1 = chunk(q, s), block_b(q, s, 0), block_b(q, s, 1)
                e = Step(q, R, NCH + s)
                k, u = c.slot(R), c.slot(2)
                pe.wait_ge(l_dst[k], 64 * c.turn(R) + 64)
                if c.reached(1):
                    pe.wait_ge(v_agg, c.at)
                forward(ps_t, g_dst[:, k, :], t_own)
                dense_1(d0)
                dense_back(d0.before(1))
                pe.wait_ge(c_xd, c.at + 1)
                pe.wait_ge(l_src[e.slot(R)], 64 * e.turn(R) + 64)
                forward(ps_t, g_src[:, e.slot(R), :], t_agg)
                if c.reached(1):
                    pe.wait_ge(v_1, c.at)
                product(ps_r, wr1[0:D, :], xd[:, u, :], p_r1)
                back_b(c.before(1))
                dense_2(d0)
                dense_1(d1)
                pe.wait_ge(c_src, c.at + 1)
                pe.wait_ge(l_ea[e.slot(R)], 16 * e.turn(R) + 16)
                if c.reached(1):
                    pe.wait_ge(v_scan, c.at)
                product(ps_m, wm2[:, :], xe[:, e.slot(R), :], p_m)
                dense_back(d0)
                pe.wait_ge(c_1, c.at + 1)
                if c.reached(1):
                    pe.wait_ge(v_2, c.at)
                product(ps_r2, wr2[0:D, :], c1d[:, u, :], p_r2)
                dense_2(d1)

            each_chunk(pe, step_b)
            dense_back(LAST_BLOCK)
            back_b(LAST_CHUNK)

        @block.scalar
        def _(act):
            act.wait_ge(s_zero, 1)
            for i in range(N * D // (P * ZCOL)):
                act.dma_start(table_z[i], zero[:, :]).then_inc(s_cleared, 16)
            act.wait_ge(s_epsc, 1)

            def copy(to, of, done):
                nc.scalar.activation(to, of, ACT.Copy).then_inc(done, 1)

            def norm_std(kind, i):
                k = 2 * kind + i.slot(2)
                act.wait_ge(ln[kind]["mv"], i.at + 1)
                if i.reached(2):
                    act.wait_ge(ln[kind]["rstd"], i.before(1).at)
                nc.scalar.activation(std[:, k, :], mv[:, k, :, 1], ACT.Sqrt,
                                     bias=epsc[:, :]).then_inc(ln[kind]["std"], 1)

            def dense_e1(d):
                act.wait_ge(d_1, d.at + 1)
                if d.reached(2):
                    act.wait_ge(d_2, d.before(1).at)
                copy(c1t[0:D, d.slot(2), :], ps_1[0:D, :], d_e1)

            def dense_e2(d):
                act.wait_ge(d_2, d.at + 1)
                if d.reached(2):
                    act.wait_ge(d_n, d.before(1).at)
                copy(c2t[:, d.slot(2), :], ps_2[0:D, :], d_e2)

            def dense_std(d):
                if d.reached(0):
                    norm_std(DENSE, d)

            def dense_norm(d):
                if d.reached(0):
                    k = d.slot(2)
                    act.wait_ge(ln[DENSE]["shift"], d.at + 1)
                    if d.reached(R):
                        act.wait_ge(o_st[d.slot(R)], 16 * d.turn(R))
                    for r in range(TPC):
                        last = nc.scalar.activation(
                            ob[:, d.slot(R), row(r)], ps_y[:, row(r)], ACT.Identity,
                            bias=shift[:, k, r:r + 1], scale=rstd[:, k, r:r + 1])
                    last.then_inc(ln[DENSE]["done"], 1)

            def step_a(q, s, last=False):
                c, d = chunk(q, s), block_a(q, s)
                k = c.slot(R)
                act.wait_ge(a_t, c.at + 1)
                if c.reached(R):
                    act.wait_ge(a_r, c.before(R - 1).at)
                copy(xe[0:D, k, :], ps_t[0:D, :], a_xe)
                dense_e1(d)
                dense_std(d.before(1))
                act.wait_ge(a_r, c.at + 1)
                if c.reached(R):
                    act.wait_ge(k_rt[k], 16 * c.turn(R))
                copy(rt1[:, k, :], ps_r[0:D, :], a_rc)
                dense_e2(d)
                dense_norm(d.before(1))
                act.wait_ge(a_n, c.at + 1)
                copy(nat[:, ds(c.at * TPC * D, TPC * D)], ps_n[:, 0:TPC * D], a_nc)

            each_chunk(act, step_a)
            act.wait_ge(a_nc, NCH)

            def step_s(q, s, last=False):
                c, d = chunk(q, s), block_s(q, s)
                if c.reached(2):
                    act.wait_ge(sc[c.slot(2)], 64 * c.turn(2))
                copy(stage[:, c.slot(2), :], nat[:, ds(c.at * TPC * D, TPC * D)], s_stage)
                dense_e1(d)
                dense_std(d.before(1))
                dense_e2(d)
                dense_norm(d.before(1))

            each_chunk(act, step_s)
            act.wait_ge(s_stage, NCH)

            def edge_rows(c):
                if c.reached(0):
                    act.wait_ge(p_n, c.at + 1)
                    copy(nat[:, ds(c.at * TPC * D, TPC * D)], ps_n[:, 0:TPC * D], c_n)

            def step_b(q, s, last=False):
                c, d0, d1 = chunk(q, s), block_b(q, s, 0), block_b(q, s, 1)
                u = c.slot(2)
                act.wait_ge(t_own, c.at + 1)
                if c.reached(2):
                    act.wait_ge(p_r1, c.before(1).at)
                    act.wait_ge(v_y, c.before(1).at)
                copy(xd[:, u, :], ps_t[0:D, :], c_xd)
                dense_e1(d0)
                dense_std(d0.before(1))
                dense_norm(d0.before(1))
                edge_rows(c.before(1))
                dense_e2(d0)
                dense_e1(d1)
                dense_std(d0)
                dense_norm(d0)
                dense_e2(d1)

            each_chunk(act, step_b)
            dense_std(LAST_BLOCK)
            dense_norm(LAST_BLOCK)
            edge_rows(LAST_CHUNK)
            each_chunk(act, lambda q, s, last=False: norm_std(EDGE, chunk(q, s)))
            act.wait_ge(s_cleared, 16 * (N * D // (P * ZCOL)))

        @block.vector
        def _(dve):
            V = nc.vector
            V.memset(zero[:, :], 0.0).then_inc(s_zero, 1)
            V.memset(epsc[:, :], EPS).then_inc(s_epsc, 1)
            V.memset(xtb[D:D + 1, :, :], 1.0).then_inc(s_ones, 1)
            V.memset(c1t[D:D + 1, :, :], 1.0).then_inc(s_ones, 1)
            dve.wait_ge(s_index, 5 * 16)
            V.tensor_tensor(row_m[:, :], row_d[:, :], row_p[:, :], ALU.is_equal).then_inc(s_prep, 1)
            V.tensor_tensor(eq_c[:, :], dst_i[:, :], dst_n[:, :], ALU.is_equal).then_inc(s_prep, 1)
            dve.wait_ge(s_prep, 2)
            V.tensor_scalar(row_m[:, :], row_m[:, :], 2.0, -1.0, ALU.mult, ALU.add).then_inc(s_prep, 1)
            V.scalar_tensor_tensor(out=end_i[:, :], in0=eq_c[:, :], scalar=float(FAR), in1=dst_i[:, :],
                                   op0=ALU.mult, op1=ALU.add).then_inc(s_prep, 1)
            V.tensor_scalar(own_i[:, :], dst_i[:, :], float(N - 1), None, ALU.min).then_inc(s_prep, 1)
            dve.wait_ge(s_prep, 5)
            V.tensor_scalar(row_m[:, :], row_m[:, :], FMAX, None, ALU.mult).then_inc(s_prep, 1)
            dve.wait_ge(s_const, 10 * 16)

            def leaky(to, of, done):
                V.scalar_tensor_tensor(out=to, in0=of, scalar=SLOPE, in1=of,
                                       op0=ALU.mult, op1=ALU.max).then_inc(done, 1)

            def scan(c, ps, mx, ring, k, mk, done):
                if c.reached(1):
                    dve.wait_ge(done, c.at)
                    first = mx[:, c.before(1).slot(ring), CH - 1:CH]
                else:
                    first = 0.0
                V.tensor_tensor_scan(mx[:, k, :], mask[:, mk, :], ps[0:D, :], first,
                                     ALU.min, ALU.max).then_inc(done, 1)

            def dense_c1(d):
                dve.wait_ge(d_e1, d.at + 1)
                leaky(c1t[0:D, d.slot(2), :], c1t[0:D, d.slot(2), :], d_c1)

            def dense_c2(d):
                dve.wait_ge(d_e2, d.at + 1)
                leaky(c2t[:, d.slot(2), :], c2t[:, d.slot(2), :], d_c2)

            def dense_x(d):
                dve.wait_ge(d_c2, d.at + 1)
                dve.wait_ge(l_xt[d.slot(R)], 16 * d.turn(R) + 16)
                t = c2t[:, d.slot(2), :]
                V.tensor_tensor(t, t, xtb[0:D, d.slot(R), :], ALU.add).then_inc(d_y, 1)

            def norm_stats(kind, i, rows):
                k = 2 * kind + i.slot(2)
                sm = ln[kind]
                if i.reached(2):
                    dve.wait_ge(sm["mv"], i.before(1).at)
                for r in range(TPC):
                    last = V.bn_stats(stat[:, k, r, :], rows(r))
                last.then_inc(sm["stats"], 1)
                dve.wait_ge(sm["stats"], i.at + 1)
                if i.reached(2):
                    dve.wait_ge(sm["done"], i.before(1).at)
                V.memset(idle[:, :], 0.0)
                for r in range(TPC):
                    last = V.bn_aggr(mv[:, k, r, :], stat[:, k, r, :])
                last.then_inc(sm["mv"], 1)

            def norm_rstd(kind, i):
                k = 2 * kind + i.slot(2)
                sm = ln[kind]
                dve.wait_ge(sm["std"], i.at + 1)
                if i.reached(2):
                    dve.wait_ge(sm["done"], i.before(1).at)
                V.reciprocal(rstd[:, k, :], std[:, k, :]).then_inc(sm["rstd"], 1)
                dve.wait_ge(sm["rstd"], i.at + 1)

            def dense_stats(d):
                if d.reached(0):
                    dve.wait_ge(d_n, d.at + 1)
                    norm_stats(DENSE, d, lambda r: ps_y[:, row(r)])

            def dense_shift(d):
                if d.reached(0):
                    k = d.slot(2)
                    norm_rstd(DENSE, d)
                    V.scalar_tensor_tensor(out=shift[:, k, :], in0=mv[:, k, :, 0], scalar=-1.0,
                                           in1=rstd[:, k, :], op0=ALU.mult, op1=ALU.mult)\
                     .then_inc(ln[DENSE]["shift"], 1)

            def step_a(q, s, last=False):
                c, d = chunk(q, s), block_a(q, s)
                k = c.slot(R)
                dense_c1(d)
                dense_stats(d.before(1))
                dve.wait_ge(a_m, c.at + 1)
                dve.wait_ge(l_mask[k], 16 * c.turn(R) + 16)
                if c.reached(R):
                    dve.wait_ge(k_mx[k], 16 * c.turn(R))
                    dve.wait_ge(a_n, c.before(R - 1).at)
                scan(c, ps_m, mx1, R, k, k, a_scan)
                dense_shift(d.before(1))
                dense_c2(d)
                dense_x(d)

            each_chunk(dve, step_a)

            def step_s(q, s, last=False):
                d = block_s(q, s)
                dense_c1(d)
                dense_stats(d.before(1))
                dense_c2(d)
                dense_shift(d.before(1))
                dense_x(d)

            each_chunk(dve, step_s)

            def step_b(q, s, last=False):
                c, d0, d1 = chunk(q, s), block_b(q, s, 0), block_b(q, s, 1)
                e = Step(q, R, NCH + s)
                k, u = c.slot(R), c.slot(2)
                dense_c1(d0)
                dense_stats(d0.before(1))
                dve.wait_ge(t_agg, c.at + 1)
                dve.wait_ge(l_rt[k], 16 * c.turn(R) + 16)
                V.scalar_tensor_tensor(out=rt1[:, k, :], in0=ps_t[0:D, :], scalar=b1c[:, 0:1],
                                       in1=rt1[:, k, :], op0=ALU.add, op1=ALU.add).then_inc(v_agg, 1)
                dense_shift(d0.before(1))
                dve.wait_ge(v_agg, c.at + 1)
                if c.reached(R):
                    dve.wait_ge(p_m, c.before(R - 1).at)
                leaky(xe[0:D, e.slot(R), :], rt1[:, k, :], c_src)
                dve.wait_ge(p_r1, c.at + 1)
                dve.wait_ge(l_mx[k], 16 * c.turn(R) + 16)
                V.scalar_tensor_tensor(out=mx1[:, k, :], in0=ps_r[0:D, :], scalar=b1c[:, 0:1],
                                       in1=mx1[:, k, :], op0=ALU.add, op1=ALU.add).then_inc(v_1, 1)
                dense_c2(d0)
                dve.wait_ge(v_1, c.at + 1)
                if c.reached(2):
                    dve.wait_ge(p_r2, c.before(1).at)
                leaky(c1d[:, u, :], mx1[:, k, :], c_1)
                dense_x(d0)
                dense_c1(d1)
                dense_stats(d0)
                dve.wait_ge(p_m, c.at + 1)
                dve.wait_ge(l_mask[e.slot(R)], 16 * e.turn(R) + 16)
                if c.reached(2):
                    dve.wait_ge(v_2, c.before(1).at)
                scan(c, ps_m, mx2, 2, u, e.slot(R), v_scan)
                dense_shift(d0)
                dve.wait_ge(p_r2, c.at + 1)
                dve.wait_ge(v_scan, c.at + 1)
                if c.reached(2):
                    dve.wait_ge(p_n, c.before(1).at)
                V.scalar_tensor_tensor(out=yd[:, u, :], in0=ps_r2[0:D, :], scalar=b2c[:, 0:1],
                                       in1=mx2[:, u, :], op0=ALU.add, op1=ALU.add).then_inc(v_2, 1)
                dense_c2(d1)
                dve.wait_ge(v_2, c.at + 1)
                leaky(yd[:, u, :], yd[:, u, :], c_2)
                dense_x(d1)
                dve.wait_ge(c_2, c.at + 1)
                V.tensor_tensor(yd[:, u, :], yd[:, u, :], xd[:, u, :], ALU.add).then_inc(v_y, 1)

            each_chunk(dve, step_b)
            dense_stats(LAST_BLOCK)
            dense_shift(LAST_BLOCK)

            def edge_norm(c):
                if c.reached(0):
                    e = Step(c.q, c.a, NCH + c.b)
                    norm_rstd(EDGE, c)
                    dve.wait_ge(sc[e.slot(2)], 64 * e.turn(2))
                    for r in range(TPC):
                        last = V.tensor_scalar(stage[:, e.slot(2), row(r)],
                                               nat[:, ds(c.at * (TPC * D) + r * D, D)],
                                               mv[:, 2 + c.slot(2), r, 0:1], rstd[:, 2 + c.slot(2), r:r + 1],
                                               ALU.subtract, ALU.mult)
                    last.then_inc(ln[EDGE]["done"], 1)

            dve.wait_ge(c_n, NCH)

            def step_n(q, s, last=False):
                c = chunk(q, s)
                norm_stats(EDGE, c, lambda r: nat[:, ds(c.at * (TPC * D) + r * D, D)])
                edge_norm(c.before(1))

            each_chunk(dve, step_n)
            edge_norm(LAST_CHUNK)


def kernel(x, src, dst, edge_attr_32, L0_gnn_W1_msg, L0_gnn_W1_edge, L0_gnn_W1_root, L0_gnn_b1,
           L0_gnn_W2_msg, L0_gnn_W2_edge, L0_gnn_W2_root, L0_gnn_b2):
    import numpy as np
    import concourse.bacc as bacc
    from concourse.bass_utils import run_bass_kernel_spmd

    x = np.ascontiguousarray(x)
    src_p = np.zeros(EP, np.int32)
    src_p[:E] = src
    dst_p = np.full(EP + 2, FAR, np.int32)
    dst_p[0] = -1
    dst_p[1:E + 1] = dst
    xt = np.zeros((NB * CH, D), np.float32)
    xt[:N] = x
    xt = xt.reshape(NB, P, TPC, D).transpose(0, 3, 2, 1).reshape(NB, D, CH)
    ea = np.zeros((EP, DE), np.float32)
    ea[:E] = edge_attr_32
    column = lambda a: a.reshape(NT, P).T
    arrays = dict(
        x=x, xt=xt, src=column(src_p), dst=column(dst_p[1:EP + 1]), dst_next=column(dst_p[2:EP + 2]),
        dst_row=dst_p[1:EP + 1].reshape(P, NT), dst_prev=dst_p[0:EP].reshape(P, NT),
        eat=ea.reshape(NCH, CH, DE).transpose(0, 2, 1),
        w1m=L0_gnn_W1_msg, w1e=L0_gnn_W1_edge, w1r=L0_gnn_W1_root, b1=np.reshape(L0_gnn_b1, (D, 1)),
        w2m=L0_gnn_W2_msg, w2e=L0_gnn_W2_edge, w2r=L0_gnn_W2_root, b2=np.reshape(L0_gnn_b2, (D, 1)))
    nc = bacc.Bacc("TRN2", target_bir_lowering=False, num_devices=1)
    feed, args = {}, {}
    for name, a in arrays.items():
        a = np.ascontiguousarray(a)
        feed[f"in_{name}"] = a
        args[name] = nc.dram_tensor(f"in_{name}", a.shape, mybir.dt.from_np(a.dtype), kind="ExternalInput").ap()
    out = nc.dram_tensor("out_0", (N, D), mybir.dt.float32, kind="ExternalOutput").ap()
    gnn_kernel(nc, **args, out=out)
    return run_bass_kernel_spmd(nc, [feed], core_ids=[0]).results[0]["out_0"]
```

```python
import concourse.bass as bass
from concourse import mybir
from contextlib import ExitStack

P = 128
N, D = 100000, 96
E, DE = 25000, 32
TPC = 4
CH = TPC * P
NCH = -(-E // CH)
EP = NCH * CH
NT = NCH * TPC
NB = -(-N // CH)
TAIL_P = (N - (NB - 1) * CH) // TPC
R = 4
FAR = 1 << 20
FMAX = 3.4028234663852886e38
EPS = 1e-5
SLOPE = 0.01
ZCOL = 1500
NZ = N * D // (P * ZCOL)
assert N * D % (P * ZCOL) == 0 and NZ == NCH + 1 and NB == 4 * NCH and NCH % R == 1


class Step:

    def __init__(self, q, a, b):
        self.q, self.a, self.b = q, a, b

    @property
    def at(self):
        return self.q * self.a + self.b

    def before(self, k):
        return Step(self.q, self.a, self.b - k)

    def slot(self, n):
        assert self.a % n == 0
        return self.b % n

    def turn(self, n):
        assert self.a % n == 0
        return self.q * (self.a // n) + self.b // n

    def reached(self, k):
        return self.a * (self.q if isinstance(self.q, int) else 1) + self.b >= k


def each_chunk(eng, step):
    for s in range(R):
        step(0, s)
    with eng.Fori(1, NCH // R) as q:
        for s in range(R):
            step(q, s)
    step(NCH // R, 0, last=True)


def chunk(q, s):
    return Step(q, R, s)


def block_a(q, s, t):
    return Step(q, 2 * R, 2 * s + t)


def block_s(q, s):
    return Step(q, R, 2 * NCH + s)


def block_b(q, s):
    return Step(q, R, 3 * NCH + s)


LAST_CHUNK = Step(NCH // R, R, 0)
LAST_BLOCK = Step(0, R, NB - 1)


def gnn_kernel(nc, x, xt, src, dst, dst_next, dst_row, dst_prev, eat,
               w1m, w1e, w1r, b1, w2m, w2e, w2r, b2, out):
    f32 = mybir.dt.float32
    i32 = mybir.dt.int32
    ALU = mybir.AluOpType
    ACT = mybir.ActivationFunctionType
    ds = bass.ds

    table = nc.dram_tensor("agg1_table", (N, D), f32, kind="Internal").ap()
    mask_row = nc.dram_tensor("mask_row", (P, NT), f32, kind="Internal").ap()
    root_keep = nc.dram_tensor("root_keep", (NCH, D, CH), f32, kind="Internal").ap()
    c1d_keep = nc.dram_tensor("c1d_keep", (NCH, D, CH), f32, kind="Internal").ap()
    xd_keep = nc.dram_tensor("xd_keep", (NCH, P, TPC * D), f32, kind="Internal").ap()
    table_z = table.rearrange("n d -> (n d)").rearrange("(k p c) -> k p c", p=P, c=ZCOL)
    mask_c = mask_row.rearrange("p t -> (p t)").rearrange("(c o e) -> c o e", o=1, e=CH)
    out_b = out[0:(NB - 1) * CH, :].rearrange("(b p j) d -> b p (j d)", p=P, j=TPC)
    out_tail = out[(NB - 1) * CH:N, :].rearrange("(p j) d -> p (j d)", j=TPC)

    ctx = ExitStack()
    with ctx:
        def sb(name, shape, dt=f32):
            return ctx.enter_context(nc.sbuf_tensor(name, shape, dt))

        def pb(name, shape):
            return ctx.enter_context(nc.psum_tensor(name, shape, f32))

        def sem(name):
            return ctx.enter_context(nc.semaphore(name))

        def sems(name, n):
            return [sem(f"{name}{i}") for i in range(n)]

        ident = sb("ident", [P, P])
        wm1 = sb("wm1", [P, D])
        wm2 = sb("wm2", [P, D])
        wr1 = sb("wr1", [D + 1, D])
        wr2 = sb("wr2", [D + 1, D])
        b1c = sb("b1c", [D, 1])
        b2c = sb("b2c", [D, 1])
        epsc = sb("epsc", [P, 1])
        zero = sb("zero", [P, ZCOL])
        gat_i = sb("gat_i", [P, 2, NT], i32)
        dst_i = sb("dst_i", [P, NT], i32)
        dst_n = sb("dst_n", [P, NT], i32)
        end_i = sb("end_i", [P, NT], i32)
        eq_c = sb("eq_c", [P, NT])
        row_d = sb("row_d", [P, NT], i32)
        row_p = sb("row_p", [P, NT], i32)
        row_m = sb("row_m", [P, NT])
        now_gat = sb("now_gat", [P, R, 2, TPC], i32)
        now_end = sb("now_end", [P, R, TPC], i32)
        g_src = sb("g_src", [P, R, TPC * D])
        g_dst = sb("g_dst", [P, R, TPC * D])
        xe = sb("xe", [P, R, CH])
        mask = sb("mask", [D, R, CH])
        mx1 = sb("mx1", [D, 2, CH])
        rt1 = sb("rt1", [D, R, CH])
        mx2 = sb("mx2", [D, 2, CH])
        xd = sb("xd", [D, 2, CH])
        c1d = sb("c1d", [D, R, CH])
        yd = sb("yd", [D, 2, CH])
        yn = sb("yn", [P, 2, TPC * D])
        nat = sb("nat", [P, NT * D])
        stage = sb("stage", [P, 2, TPC * D])
        xtb = sb("xtb", [D + 1, R, CH])
        c1t = sb("c1t", [D + 1, 2, CH])
        c2t = sb("c2t", [D, 2, CH])
        ob = sb("ob", [P, R, TPC * D])
        stat = sb("stat", [P, 4, TPC, 6])
        mv = sb("mv", [P, 4, TPC, 2])
        std = sb("std", [P, 4, TPC])
        rstd = sb("rstd", [P, 4, TPC])
        shift = sb("shift", [P, 2, TPC])
        idle = sb("idle", [1, 1])

        ps_t = pb("ps_t", [P, CH])
        ps_m = pb("ps_m", [P, CH])
        ps_r = pb("ps_r", [P, CH])
        ps_n = pb("ps_n", [P, CH])
        ps_1 = pb("ps_1", [P, CH])
        ps_2 = pb("ps_2", [P, CH])
        ps_y = [pb(f"ps_y{k}", [P, CH]) for k in range(2)]

        s_const = sem("s_const")
        s_index = sem("s_index")
        s_ident0 = sem("s_ident0")
        s_ident = sem("s_ident")
        s_zero = sem("s_zero")
        s_epsc = sem("s_epsc")
        s_ones = sem("s_ones")
        s_prep = sem("s_prep")
        s_mask_w = sem("s_mask_w")
        s_cleared = sem("s_cleared")
        l_src = sems("l_src", R)
        l_dst = sems("l_dst", R)
        l_ea = sems("l_ea", R)
        l_mask = sems("l_mask", R)
        l_xt = sems("l_xt", R)
        l_rt = sems("l_rt", R)
        l_c1d = sems("l_c1d", R)
        l_xd = sems("l_xd", R)
        k_rt = sems("k_rt", R)
        k_c1d = sems("k_c1d", R)
        k_xd = sems("k_xd", R)
        o_st = sems("o_st", R)
        sc = sems("sc", 2)
        s_now = sem("s_now")
        a_t = sem("a_t")
        a_xe = sem("a_xe")
        a_m = sem("a_m")
        a_scan = sem("a_scan")
        a_r = sem("a_r")
        a_rc = sem("a_rc")
        a_n = sem("a_n")
        a_nc = sem("a_nc")
        s_stage = sem("s_stage")
        a_own = sem("a_own")
        a_xd = sem("a_xd")
        a_r1 = sem("a_r1")
        a_z1 = sem("a_z1")
        a_c1 = sem("a_c1")
        b_t = sem("b_t")
        b_z1 = sem("b_z1")
        b_c1 = sem("b_c1")
        b_m = sem("b_m")
        b_scan = sem("b_scan")
        b_r = sem("b_r")
        b_z2 = sem("b_z2")
        b_n = sem("b_n")
        b_nc = sem("b_nc")
        e_c2 = sem("e_c2")
        e_y = sem("e_y")
        d_1 = sem("d_1")
        d_e1 = sem("d_e1")
        d_c1 = sem("d_c1")
        d_2 = sem("d_2")
        d_e2 = sem("d_e2")
        d_c2 = sem("d_c2")
        d_y = sem("d_y")
        d_n = sem("d_n")
        ln = [dict(stats=sem(f"ln_stats{k}"), mv=sem(f"ln_mv{k}"), std=sem(f"ln_std{k}"),
                   rstd=sem(f"ln_rstd{k}"), shift=sem(f"ln_shift{k}"), done=sem(f"ln_done{k}")) for k in "de"]
        DENSE, EDGE = 0, 1

        block = ctx.enter_context(nc.Block())

        def cols(j):
            return slice(j * P, (j + 1) * P)

        def row(j):
            return slice(j * D, (j + 1) * D)

        @block.gpsimd
        def _(pool):
            nc.gpsimd.memset(ident[:, :], 0.0).then_inc(s_ident0, 1)
            pool.wait_ge(s_ident0, 1)
            nc.gpsimd.affine_select(out=ident[:, :], in_=ident[:, :], compare_op=ALU.not_equal,
                                    fill=1.0, base=0, pattern=[[-1, P]],
                                    channel_multiplier=1).then_inc(s_ident, 1)

            def gather(rows, where, which, c, e, landed):
                for r in range(TPC):
                    nc.gpsimd.indirect_dma_start(
                        out=where[:, e.slot(R), row(r)], out_offset=None, in_=rows,
                        in_offset=bass.IndirectOffsetOnAxis(ap=now_gat[:, c.slot(R), which, r:r + 1], axis=0),
                    ).then_inc(landed[e.slot(R)], 16)

            def scatter(rows, c, k):
                for r in range(TPC):
                    nc.gpsimd.indirect_dma_start(
                        out=rows,
                        out_offset=bass.IndirectOffsetOnAxis(ap=now_end[:, c.slot(R), r:r + 1], axis=0),
                        in_=stage[:, k, row(r)], in_offset=None, bounds_check=N - 1,
                        oob_is_err=False).then_inc(sc[k], 16)

            pool.wait_ge(s_index, 5 * 16)
            pool.wait_ge(s_prep, 6)

            def stage_gather(c):
                nc.gpsimd.tensor_copy(now_gat[:, c.slot(R), :, :], gat_i[:, :, ds(c.at * TPC, TPC)])\
                  .then_inc(s_now, 1)

            def stage_end(c):
                nc.gpsimd.tensor_copy(now_end[:, c.slot(R), :], end_i[:, ds(c.at * TPC, TPC)])\
                  .then_inc(s_now, 1)

            stage_gather(chunk(0, 0))

            def gather_a(q, s, last=False):
                c = chunk(q, s)
                if c.reached(R - 1):
                    f = c.before(R - 1)
                    pool.wait_ge(l_src[f.slot(R)], 64 * f.turn(R) + 64)
                    pool.wait_ge(l_dst[f.slot(R)], 64 * f.turn(R) + 64)
                if c.reached(R):
                    pool.wait_ge(a_t, c.before(R - 1).at)
                    pool.wait_ge(a_own, c.before(R - 1).at)
                    pool.wait_ge(k_xd[c.slot(R)], 16 * c.turn(R))
                pool.wait_ge(s_now, c.at + 1)
                if not last:
                    stage_gather(chunk(q, s + 1))
                gather(x, g_src, 0, c, c, l_src)
                gather(x, g_dst, 1, c, c, l_dst)

            each_chunk(pool, gather_a)
            pool.wait_ge(s_cleared, 16 * NZ)

            def scatter_all(rows, base_stage, base_now, staged):
                stage_end(chunk(0, 0))

                def go(q, s, last=False):
                    c = chunk(q, s)
                    e = Step(q, R, base_stage + s)
                    if e.reached(R - 1):
                        f = e.before(R - 1)
                        pool.wait_ge(sc[f.slot(2)], 64 * f.turn(2) + 64)
                    pool.wait_ge(staged, c.at + 1)
                    pool.wait_ge(s_now, c.at + base_now + 1)
                    if not last:
                        stage_end(chunk(q, s + 1))
                    scatter(rows, c, e.slot(2))

                each_chunk(pool, go)

            scatter_all(table, 0, NCH, s_stage)
            for k in range(2):
                pool.wait_ge(sc[k], 64 * ((NCH + 1 - k) // 2))
            for k in range(R):
                pool.wait_ge(l_src[k], 64 * ((NCH + R - 1 - k) // R))
                pool.wait_ge(l_dst[k], 64 * ((NCH + R - 1 - k) // R))
            pool.wait_ge(a_t, NCH)
            stage_gather(chunk(0, 0))

            def gather_b(q, s, last=False):
                c = chunk(q, s)
                e = Step(q, R, NCH + s)
                if c.reached(R - 1):
                    f = e.before(R - 1)
                    pool.wait_ge(l_src[f.slot(R)], 64 * f.turn(R) + 64)
                if c.reached(R):
                    pool.wait_ge(b_t, c.before(R - 1).at)
                pool.wait_ge(s_now, c.at + 2 * NCH + 1)
                if not last:
                    stage_gather(chunk(q, s + 1))
                gather(table, g_src, 0, c, e, l_src)

            each_chunk(pool, gather_b)
            for k in range(R):
                pool.wait_ge(o_st[k], 16 * ((NB + R - 1 - k) // R))
            scatter_all(out, NCH, 3 * NCH, ln[EDGE]["done"])
            for k in range(2):
                pool.wait_ge(sc[k], 64 * ((2 * NCH + 1 - k) // 2))

        @block.sync
        def _(sp):
            sp.dma_start(gat_i[:, 0, :], src).then_inc(s_index, 16)
            sp.dma_start(dst_i[:, :], dst).then_inc(s_index, 16)
            sp.dma_start(dst_n[:, :], dst_next).then_inc(s_index, 16)
            sp.dma_start(row_d[:, :], dst_row).then_inc(s_index, 16)
            sp.dma_start(row_p[:, :], dst_prev).then_inc(s_index, 16)
            for to, of in ((wm1[0:D, :], w1m), (wm1[D:P, :], w1e), (wr1[0:D, :], w1r), (b1c[:, :], b1),
                           (wm2[0:D, :], w2m), (wm2[D:P, :], w2e), (wr2[0:D, :], w2r), (b2c[:, :], b2),
                           (wr1[D:D + 1, :], b1.rearrange("d o -> o d")),
                           (wr2[D:D + 1, :], b2.rearrange("d o -> o d"))):
                sp.dma_start(to, of).then_inc(s_const, 16)
            sp.wait_ge(s_prep, 6)
            sp.dma_start(mask_row, row_m[:, :]).then_inc(s_mask_w, 16)
            sp.wait_ge(s_mask_w, 16)

            def load_block(d):
                if d.reached(R):
                    sp.wait_ge(d_y, d.before(R - 1).at)
                sp.dma_start(xtb[0:D, d.slot(R), :], xt[ds(d.at, 1), :, :].rearrange("o d e -> d (o e)"))\
                  .then_inc(l_xt[d.slot(R)], 16)

            def store_block(d):
                if d.reached(0):
                    sp.wait_ge(ln[DENSE]["done"], d.at + 1)
                    sp.dma_start(out_b[ds(d.at, 1), :, :].rearrange("o p f -> p (o f)"),
                                 ob[:, d.slot(R), :]).then_inc(o_st[d.slot(R)], 16)

            def load_edges(c, e, used, scanned):
                k = e.slot(R)
                if c.reached(R):
                    sp.wait_ge(used, c.before(R - 1).at)
                    sp.wait_ge(scanned, c.before(R - 1).at)
                sp.dma_start(xe[D:P, k, :], eat[ds(c.at, 1), :, :].rearrange("o d e -> d (o e)"))\
                  .then_inc(l_ea[k], 16)
                sp.dma_start(mask[:, k, :],
                             mask_c[ds(c.at, 1), :, :].rearrange("c o e -> (c o) e").to_broadcast([D, CH]))\
                  .then_inc(l_mask[k], 16)

            def keep(where, c, what, ready, kept):
                if c.reached(0):
                    k = c.slot(R)
                    sp.wait_ge(ready, c.at + 1)
                    sp.dma_start(where[ds(c.at, 1), :, :].rearrange("o d e -> d (o e)"), what[:, k, :])\
                      .then_inc(kept[k], 16)

            def back(where, c, what, read, landed):
                k = c.slot(R)
                if c.reached(R):
                    sp.wait_ge(read, c.before(R - 1).at)
                sp.dma_start(what[:, k, :], where[ds(c.at, 1), :, :].rearrange("o d e -> d (o e)"))\
                  .then_inc(landed[k], 16)

            def keep_own(c):
                if c.reached(0):
                    k = c.slot(R)
                    sp.wait_ge(l_dst[k], 64 * c.turn(R) + 64)
                    sp.dma_start(xd_keep[ds(c.at, 1), :, :].rearrange("o d e -> d (o e)"), g_dst[:, k, :])\
                      .then_inc(k_xd[k], 16)

            def step_a(q, s, last=False):
                c, d0, d1 = chunk(q, s), block_a(q, s, 0), block_a(q, s, 1)
                load_edges(c, c, a_r, a_scan)
                load_block(d0)
                store_block(d0.before(R))
                keep_own(c.before(1))
                keep(root_keep, c.before(2), rt1, a_rc, k_rt)
                load_block(d1)
                store_block(d1.before(R))
                keep(c1d_keep, c.before(2), c1d, a_c1, k_c1d)

            each_chunk(sp, step_a)
            keep_own(LAST_CHUNK)
            for i in (1, 0):
                keep(root_keep, LAST_CHUNK.before(i), rt1, a_rc, k_rt)
                keep(c1d_keep, LAST_CHUNK.before(i), c1d, a_c1, k_c1d)

            def step_s(q, s, last=False):
                d = block_s(q, s)
                load_block(d)
                store_block(d.before(R))

            each_chunk(sp, step_s)
            for k in range(R):
                for kept in (k_rt, k_c1d, k_xd):
                    sp.wait_ge(kept[k], 16 * ((NCH + R - 1 - k) // R))
            sp.wait_ge(a_r, NCH)

            def step_b(q, s, last=False):
                c, d = chunk(q, s), block_b(q, s)
                back(root_keep, c, rt1, b_c1, l_rt)
                back(c1d_keep, c, c1d, b_r, l_c1d)
                load_block(d)
                load_edges(c, Step(q, R, NCH + s), b_m, b_scan)
                store_block(d.before(R))

            each_chunk(sp, step_b)
            for i in range(R - 1, 0, -1):
                store_block(LAST_BLOCK.before(i))
            sp.wait_ge(ln[DENSE]["done"], NB)
            sp.dma_start(out_tail, ob[0:TAIL_P, LAST_BLOCK.slot(R), :])\
              .then_inc(o_st[LAST_BLOCK.slot(R)], 16)
            sp.wait_ge(a_own, NCH)
            each_chunk(sp, lambda q, s, last=False: back(xd_keep, chunk(q, s), g_dst, e_y, l_xd))
            for k in range(R):
                sp.wait_ge(o_st[k], 16 * ((NB + R - 1 - k) // R))

        @block.tensor
        def _(pe):
            pe.wait_ge(s_ident, 1)
            pe.wait_ge(s_const, 10 * 16)
            pe.wait_ge(s_ones, 2)

            def forward(ps, rows, done):
                for r in range(TPC):
                    last = nc.tensor.transpose(ps[0:D, cols(r)], rows[:, row(r)], ident[:, :])
                last.then_inc(done, 1)

            def back(ps, t, done):
                for r in range(TPC):
                    last = nc.tensor.transpose(ps[:, row(r)], t[:, cols(r)], ident[0:D, 0:D])
                last.then_inc(done, 1)

            def product(ps, w, t, done):
                nc.tensor.matmul(ps[0:D, :], w, t, start=True, stop=True).then_inc(done, 1)

            def dense_1(d):
                pe.wait_ge(l_xt[d.slot(R)], 16 * d.turn(R) + 16)
                if d.reached(1):
                    pe.wait_ge(d_e1, d.at)
                product(ps_1, wr1[:, :], xtb[:, d.slot(R), :], d_1)

            def dense_2(d):
                pe.wait_ge(d_c1, d.at + 1)
                if d.reached(1):
                    pe.wait_ge(d_e2, d.at)
                product(ps_2, wr2[:, :], c1t[:, d.slot(2), :], d_2)

            def dense_2b(d):
                if d.reached(0):
                    dense_2(d)

            def dense_back(d):
                if d.reached(0):
                    pe.wait_ge(d_y, d.at + 1)
                    if d.reached(2):
                        pe.wait_ge(ln[DENSE]["done"], d.before(1).at)
                    back(ps_y[d.slot(2)], c2t[:, d.slot(2), :], d_n)

            def maxima_back(c):
                if c.reached(0):
                    pe.wait_ge(a_scan, c.at + 1)
                    if c.reached(1):
                        pe.wait_ge(a_nc, c.at)
                    back(ps_n, mx1[:, c.slot(2), :], a_n)

            def step_a(q, s, last=False):
                c, d0, d1 = chunk(q, s), block_a(q, s, 0), block_a(q, s, 1)
                k, u = c.slot(R), c.slot(2)
                pe.wait_ge(l_src[k], 64 * c.turn(R) + 64)
                if c.reached(1):
                    pe.wait_ge(a_xd, c.at)
                forward(ps_t, g_src[:, k, :], a_t)
                dense_1(d0)
                dense_2b(d0.before(1))
                pe.wait_ge(l_dst[k], 64 * c.turn(R) + 64)
                pe.wait_ge(a_xe, c.at + 1)
                forward(ps_t, g_dst[:, k, :], a_own)
                maxima_back(c.before(1))
                dense_back(d0.before(2))
                pe.wait_ge(l_ea[k], 16 * c.turn(R) + 16)
                if c.reached(1):
                    pe.wait_ge(a_scan, c.at)
                product(ps_m, wm1[:, :], xe[:, k, :], a_m)
                if c.reached(1):
                    pe.wait_ge(a_z1, c.at)
                product(ps_r, wr1[0:D, :], xe[0:D, k, :], a_r)
                dense_1(d1)
                dense_2(d0)
                pe.wait_ge(a_xd, c.at + 1)
                pe.wait_ge(a_rc, c.at + 1)
                product(ps_r, wr1[0:D, :], xd[:, u, :], a_r1)
                dense_back(d1.before(2))

            each_chunk(pe, step_a)

            def step_s(q, s, last=False):
                d = block_s(q, s)
                dense_1(d)
                dense_2(d.before(1))
                dense_back(d.before(2))

            maxima_back(LAST_CHUNK)
            each_chunk(pe, step_s)
            pe.wait_ge(a_xd, NCH)
            pe.wait_ge(a_z1, NCH)
            pe.wait_ge(a_nc, NCH)

            def sums_back(c):
                if c.reached(0):
                    pe.wait_ge(b_z2, c.at + 1)
                    if c.reached(1):
                        pe.wait_ge(b_nc, c.at)
                    back(ps_n, yd[:, c.slot(2), :], b_n)

            def step_b(q, s, last=False):
                c, d = chunk(q, s), block_b(q, s)
                e = Step(q, R, NCH + s)
                k = c.slot(R)
                pe.wait_ge(l_src[e.slot(R)], 64 * e.turn(R) + 64)
                if c.reached(1):
                    pe.wait_ge(b_z1, c.at)
                forward(ps_t, g_src[:, e.slot(R), :], b_t)
                dense_1(d)
                dense_2(d.before(1))
                pe.wait_ge(l_c1d[k], 16 * c.turn(R) + 16)
                if c.reached(1):
                    pe.wait_ge(b_z2, c.at)
                product(ps_r, wr2[0:D, :], c1d[:, k, :], b_r)
                sums_back(c.before(1))
                dense_back(d.before(2))
                pe.wait_ge(b_c1, c.at + 1)
                pe.wait_ge(l_ea[e.slot(R)], 16 * e.turn(R) + 16)
                if c.reached(1):
                    pe.wait_ge(b_scan, c.at)
                product(ps_m, wm2[:, :], xe[:, e.slot(R), :], b_m)

            each_chunk(pe, step_b)
            dense_2(LAST_BLOCK)
            dense_back(LAST_BLOCK.before(1))
            dense_back(LAST_BLOCK)
            sums_back(LAST_CHUNK)

        @block.scalar
        def _(act):
            act.wait_ge(s_zero, 1)
            act.wait_ge(s_epsc, 1)

            def clear(i):
                act.dma_start(table_z[ds(i, 1), :, :].rearrange("o p c -> p (o c)"), zero[:, :])\
                   .then_inc(s_cleared, 16)

            def copy(to, of, done):
                nc.scalar.activation(to, of, ACT.Copy).then_inc(done, 1)

            def norm_std(kind, i):
                k = 2 * kind + i.slot(2)
                act.wait_ge(ln[kind]["mv"], i.at + 1)
                if i.reached(2):
                    act.wait_ge(ln[kind]["rstd"], i.before(1).at)
                nc.scalar.activation(std[:, k, :], mv[:, k, :, 1], ACT.Sqrt,
                                     bias=epsc[:, :]).then_inc(ln[kind]["std"], 1)

            def dense_e1(d):
                act.wait_ge(d_1, d.at + 1)
                if d.reached(2):
                    act.wait_ge(d_2, d.before(1).at)
                copy(c1t[0:D, d.slot(2), :], ps_1[0:D, :], d_e1)

            def dense_e2(d):
                if not d.reached(0):
                    return
                act.wait_ge(d_2, d.at + 1)
                if d.reached(2):
                    act.wait_ge(d_n, d.before(1).at)
                copy(c2t[:, d.slot(2), :], ps_2[0:D, :], d_e2)

            def dense_std(d):
                if d.reached(0):
                    norm_std(DENSE, d)

            def dense_norm(d):
                if d.reached(0):
                    k = d.slot(2)
                    act.wait_ge(ln[DENSE]["shift"], d.at + 1)
                    if d.reached(R):
                        act.wait_ge(o_st[d.slot(R)], 16 * d.turn(R))
                    for r in range(TPC):
                        last = nc.scalar.activation(
                            ob[:, d.slot(R), row(r)], ps_y[k][:, row(r)], ACT.Identity,
                            bias=shift[:, k, r:r + 1], scale=rstd[:, k, r:r + 1])
                    last.then_inc(ln[DENSE]["done"], 1)

            def maxima(c):
                if c.reached(0):
                    act.wait_ge(a_n, c.at + 1)
                    copy(nat[:, ds(c.at * TPC * D, TPC * D)], ps_n[:, 0:TPC * D], a_nc)

            def step_a(q, s, last=False):
                c, d0, d1 = chunk(q, s), block_a(q, s, 0), block_a(q, s, 1)
                k, u = c.slot(R), c.slot(2)
                act.wait_ge(a_t, c.at + 1)
                if c.reached(R):
                    act.wait_ge(a_r, c.before(R - 1).at)
                copy(xe[0:D, k, :], ps_t[0:D, :], a_xe)
                clear(c.at)
                dense_e1(d0)
                dense_e2(d0.before(1))
                act.wait_ge(a_own, c.at + 1)
                if c.reached(2):
                    act.wait_ge(a_r1, c.before(1).at)
                copy(xd[:, u, :], ps_t[0:D, :], a_xd)
                maxima(c.before(1))
                dense_norm(d0.before(3))
                dense_std(d0.before(2))
                act.wait_ge(a_r, c.at + 1)
                if c.reached(R):
                    act.wait_ge(k_rt[k], 16 * c.turn(R))
                copy(rt1[:, k, :], ps_r[0:D, :], a_rc)
                dense_e1(d1)
                dense_e2(d0)
                dense_norm(d1.before(3))
                dense_std(d1.before(2))

            each_chunk(act, step_a)
            clear(NZ - 1)
            maxima(LAST_CHUNK)
            act.wait_ge(a_nc, NCH)

            def step_s(q, s, last=False):
                c, d = chunk(q, s), block_s(q, s)
                if c.reached(2):
                    act.wait_ge(sc[c.slot(2)], 64 * c.turn(2))
                copy(stage[:, c.slot(2), :], nat[:, ds(c.at * TPC * D, TPC * D)], s_stage)
                dense_e1(d)
                dense_e2(d.before(1))
                dense_norm(d.before(3))
                dense_std(d.before(2))

            each_chunk(act, step_s)
            act.wait_ge(s_stage, NCH)

            def sums(c):
                if c.reached(0):
                    act.wait_ge(b_n, c.at + 1)
                    copy(nat[:, ds(c.at * TPC * D, TPC * D)], ps_n[:, 0:TPC * D], b_nc)

            def step_b(q, s, last=False):
                d = block_b(q, s)
                dense_e1(d)
                dense_e2(d.before(1))
                dense_norm(d.before(3))
                sums(chunk(q, s).before(1))
                dense_std(d.before(2))

            each_chunk(act, step_b)
            dense_e2(LAST_BLOCK)
            dense_norm(LAST_BLOCK.before(2))
            dense_std(LAST_BLOCK.before(1))
            dense_norm(LAST_BLOCK.before(1))
            dense_std(LAST_BLOCK)
            dense_norm(LAST_BLOCK)
            sums(LAST_CHUNK)
            each_chunk(act, lambda q, s, last=False: norm_std(EDGE, chunk(q, s)))
            act.wait_ge(s_cleared, 16 * NZ)

        @block.vector
        def _(dve):
            V = nc.vector
            V.memset(zero[:, :], 0.0).then_inc(s_zero, 1)
            V.memset(epsc[:, :], EPS).then_inc(s_epsc, 1)
            V.memset(xtb[D:D + 1, :, :], 1.0).then_inc(s_ones, 1)
            V.memset(c1t[D:D + 1, :, :], 1.0).then_inc(s_ones, 1)
            dve.wait_ge(s_index, 5 * 16)
            V.tensor_tensor(row_m[:, :], row_d[:, :], row_p[:, :], ALU.is_equal).then_inc(s_prep, 1)
            V.tensor_tensor(eq_c[:, :], dst_i[:, :], dst_n[:, :], ALU.is_equal).then_inc(s_prep, 1)
            dve.wait_ge(s_prep, 2)
            V.tensor_scalar(row_m[:, :], row_m[:, :], 2.0, -1.0, ALU.mult, ALU.add).then_inc(s_prep, 1)
            V.scalar_tensor_tensor(out=end_i[:, :], in0=eq_c[:, :], scalar=float(FAR), in1=dst_i[:, :],
                                   op0=ALU.mult, op1=ALU.add).then_inc(s_prep, 1)
            V.tensor_scalar(gat_i[:, 1, :], dst_i[:, :], float(N - 1), None, ALU.min).then_inc(s_prep, 1)
            dve.wait_ge(s_prep, 5)
            V.tensor_scalar(row_m[:, :], row_m[:, :], FMAX, None, ALU.mult).then_inc(s_prep, 1)
            dve.wait_ge(s_const, 10 * 16)

            def leaky(to, of, done):
                V.scalar_tensor_tensor(out=to, in0=of, scalar=SLOPE, in1=of,
                                       op0=ALU.mult, op1=ALU.max).then_inc(done, 1)

            def scan(c, mx, mk, done):
                if c.reached(1):
                    dve.wait_ge(done, c.at)
                    first = mx[:, c.before(1).slot(2), CH - 1:CH]
                else:
                    first = 0.0
                V.tensor_tensor_scan(mx[:, c.slot(2), :], mask[:, mk, :], ps_m[0:D, :], first,
                                     ALU.min, ALU.max).then_inc(done, 1)

            def dense_c1(d):
                dve.wait_ge(d_e1, d.at + 1)
                leaky(c1t[0:D, d.slot(2), :], c1t[0:D, d.slot(2), :], d_c1)

            def dense_c2(d):
                if not d.reached(0):
                    return
                dve.wait_ge(d_e2, d.at + 1)
                leaky(c2t[:, d.slot(2), :], c2t[:, d.slot(2), :], d_c2)

            def dense_x(d):
                if not d.reached(0):
                    return
                dve.wait_ge(d_c2, d.at + 1)
                dve.wait_ge(l_xt[d.slot(R)], 16 * d.turn(R) + 16)
                t = c2t[:, d.slot(2), :]
                V.tensor_tensor(t, t, xtb[0:D, d.slot(R), :], ALU.add).then_inc(d_y, 1)

            def norm_stats(kind, i, rows):
                k = 2 * kind + i.slot(2)
                sm = ln[kind]
                if i.reached(2):
                    dve.wait_ge(sm["mv"], i.before(1).at)
                for r in range(TPC):
                    last = V.bn_stats(stat[:, k, r, :], rows(r))
                last.then_inc(sm["stats"], 1)
                dve.wait_ge(sm["stats"], i.at + 1)
                if i.reached(2):
                    dve.wait_ge(sm["done"], i.before(1).at)
                V.memset(idle[:, :], 0.0)
                for r in range(TPC):
                    last = V.bn_aggr(mv[:, k, r, :], stat[:, k, r, :])
                last.then_inc(sm["mv"], 1)

            def norm_rstd(kind, i):
                k = 2 * kind + i.slot(2)
                sm = ln[kind]
                dve.wait_ge(sm["std"], i.at + 1)
                if i.reached(2):
                    dve.wait_ge(sm["done"], i.before(1).at)
                V.reciprocal(rstd[:, k, :], std[:, k, :]).then_inc(sm["rstd"], 1)
                dve.wait_ge(sm["rstd"], i.at + 1)

            def dense_stats(d):
                if d.reached(0):
                    dve.wait_ge(d_n, d.at + 1)
                    norm_stats(DENSE, d, lambda r: ps_y[d.slot(2)][:, row(r)])

            def dense_shift(d):
                if d.reached(0):
                    k = d.slot(2)
                    norm_rstd(DENSE, d)
                    V.scalar_tensor_tensor(out=shift[:, k, :], in0=mv[:, k, :, 0], scalar=-1.0,
                                           in1=rstd[:, k, :], op0=ALU.mult, op1=ALU.mult)\
                     .then_inc(ln[DENSE]["shift"], 1)

            def step_a(q, s, last=False):
                c, d0, d1 = chunk(q, s), block_a(q, s, 0), block_a(q, s, 1)
                k, u = c.slot(R), c.slot(2)
                dense_shift(d0.before(3))
                dense_c1(d0)
                dense_c2(d0.before(1))
                dense_x(d0.before(1))
                dense_stats(d0.before(2))
                dve.wait_ge(a_m, c.at + 1)
                dve.wait_ge(l_mask[k], 16 * c.turn(R) + 16)
                if c.reached(2):
                    dve.wait_ge(a_n, c.before(1).at)
                    dve.wait_ge(a_z1, c.before(1).at)
                scan(c, mx1, k, a_scan)
                dense_shift(d1.before(3))
                dense_c1(d1)
                dense_c2(d0)
                dense_x(d0)
                dve.wait_ge(a_r1, c.at + 1)
                dve.wait_ge(a_scan, c.at + 1)
                if c.reached(R):
                    dve.wait_ge(k_c1d[k], 16 * c.turn(R))
                V.scalar_tensor_tensor(out=c1d[:, k, :], in0=ps_r[0:D, :], scalar=b1c[:, 0:1],
                                       in1=mx1[:, u, :], op0=ALU.add, op1=ALU.add).then_inc(a_z1, 1)
                dense_stats(d1.before(2))
                dve.wait_ge(a_z1, c.at + 1)
                leaky(c1d[:, k, :], c1d[:, k, :], a_c1)

            each_chunk(dve, step_a)

            def step_s(q, s, last=False):
                d = block_s(q, s)
                dense_shift(d.before(3))
                dense_c1(d)
                dense_c2(d.before(1))
                dense_stats(d.before(2))
                dense_x(d.before(1))

            each_chunk(dve, step_s)

            def step_b(q, s, last=False):
                c, d = chunk(q, s), block_b(q, s)
                e = Step(q, R, NCH + s)
                k, u = c.slot(R), c.slot(2)
                dense_shift(d.before(3))
                dve.wait_ge(b_t, c.at + 1)
                dve.wait_ge(l_rt[k], 16 * c.turn(R) + 16)
                V.scalar_tensor_tensor(out=rt1[:, k, :], in0=ps_t[0:D, :], scalar=b1c[:, 0:1],
                                       in1=rt1[:, k, :], op0=ALU.add, op1=ALU.add).then_inc(b_z1, 1)
                dense_c1(d)
                dve.wait_ge(b_z1, c.at + 1)
                if c.reached(R):
                    dve.wait_ge(b_m, c.before(R - 1).at)
                leaky(xe[0:D, e.slot(R), :], rt1[:, k, :], b_c1)
                dense_c2(d.before(1))
                dense_x(d.before(1))
                dense_stats(d.before(2))
                dve.wait_ge(b_m, c.at + 1)
                dve.wait_ge(l_mask[e.slot(R)], 16 * e.turn(R) + 16)
                if c.reached(2):
                    dve.wait_ge(b_z2, c.before(1).at)
                scan(c, mx2, e.slot(R), b_scan)
                dve.wait_ge(b_r, c.at + 1)
                dve.wait_ge(b_scan, c.at + 1)
                if c.reached(2):
                    dve.wait_ge(b_n, c.before(1).at)
                V.scalar_tensor_tensor(out=yd[:, u, :], in0=ps_r[0:D, :], scalar=b2c[:, 0:1],
                                       in1=mx2[:, u, :], op0=ALU.add, op1=ALU.add).then_inc(b_z2, 1)

            each_chunk(dve, step_b)
            dense_shift(LAST_BLOCK.before(2))
            dense_c2(LAST_BLOCK)
            dense_x(LAST_BLOCK)
            dense_stats(LAST_BLOCK.before(1))
            dense_shift(LAST_BLOCK.before(1))
            dense_stats(LAST_BLOCK)
            dense_shift(LAST_BLOCK)

            def edge_norm(c):
                if c.reached(0):
                    e = Step(c.q, c.a, NCH + c.b)
                    norm_rstd(EDGE, c)
                    dve.wait_ge(sc[e.slot(2)], 64 * e.turn(2))
                    for r in range(TPC):
                        last = V.tensor_scalar(stage[:, e.slot(2), row(r)], yn[:, c.slot(2), row(r)],
                                               mv[:, 2 + c.slot(2), r, 0:1], rstd[:, 2 + c.slot(2), r:r + 1],
                                               ALU.subtract, ALU.mult)
                    last.then_inc(ln[EDGE]["done"], 1)

            dve.wait_ge(b_nc, NCH)

            def step_n(q, s, last=False):
                c = chunk(q, s)
                u, k = c.slot(2), c.slot(R)
                if c.reached(2):
                    dve.wait_ge(ln[EDGE]["done"], c.before(1).at)
                z = nat[:, ds(c.at * TPC * D, TPC * D)]
                V.scalar_tensor_tensor(out=yn[:, u, :], in0=z, scalar=SLOPE, in1=z,
                                       op0=ALU.mult, op1=ALU.max).then_inc(e_c2, 1)
                edge_norm(c.before(1))
                dve.wait_ge(e_c2, c.at + 1)
                dve.wait_ge(l_xd[k], 16 * c.turn(R) + 16)
                V.tensor_tensor(yn[:, u, :], yn[:, u, :], g_dst[:, k, :], ALU.add).then_inc(e_y, 1)
                dve.wait_ge(e_y, c.at + 1)
                norm_stats(EDGE, c, lambda r: yn[:, u, row(r)])

            each_chunk(dve, step_n)
            edge_norm(LAST_CHUNK)


def kernel(x, src, dst, edge_attr_32, L0_gnn_W1_msg, L0_gnn_W1_edge, L0_gnn_W1_root, L0_gnn_b1,
           L0_gnn_W2_msg, L0_gnn_W2_edge, L0_gnn_W2_root, L0_gnn_b2):
    import numpy as np
    import concourse.bacc as bacc
    from concourse.bass_utils import run_bass_kernel_spmd

    x = np.ascontiguousarray(x)
    src_p = np.zeros(EP, np.int32)
    src_p[:E] = src
    dst_p = np.full(EP + 2, FAR, np.int32)
    dst_p[0] = -1
    dst_p[1:E + 1] = dst
    xt = np.zeros((NB * CH, D), np.float32)
    xt[:N] = x
    xt = xt.reshape(NB, P, TPC, D).transpose(0, 3, 2, 1).reshape(NB, D, CH)
    ea = np.zeros((EP, DE), np.float32)
    ea[:E] = edge_attr_32
    column = lambda a: a.reshape(NT, P).T
    arrays = dict(
        x=x, xt=xt, src=column(src_p), dst=column(dst_p[1:EP + 1]), dst_next=column(dst_p[2:EP + 2]),
        dst_row=dst_p[1:EP + 1].reshape(P, NT), dst_prev=dst_p[0:EP].reshape(P, NT),
        eat=ea.reshape(NCH, CH, DE).transpose(0, 2, 1),
        w1m=L0_gnn_W1_msg, w1e=L0_gnn_W1_edge, w1r=L0_gnn_W1_root, b1=np.reshape(L0_gnn_b1, (D, 1)),
        w2m=L0_gnn_W2_msg, w2e=L0_gnn_W2_edge, w2r=L0_gnn_W2_root, b2=np.reshape(L0_gnn_b2, (D, 1)))
    nc = bacc.Bacc("TRN2", target_bir_lowering=False, num_devices=1)
    feed, args = {}, {}
    for name, a in arrays.items():
        a = np.ascontiguousarray(a)
        feed[f"in_{name}"] = a
        args[name] = nc.dram_tensor(f"in_{name}", a.shape, mybir.dt.from_np(a.dtype), kind="ExternalInput").ap()
    out = nc.dram_tensor("out_0", (N, D), mybir.dt.float32, kind="ExternalOutput").ap()
    gnn_kernel(nc, **args, out=out)
    return run_bass_kernel_spmd(nc, [feed], core_ids=[0]).results[0]["out_0"]
```

```python
import concourse.bass as bass
from concourse import mybir
from contextlib import ExitStack

P = 128
N, D = 100000, 96
E, DE = 25000, 32
TPC = 4
CH = TPC * P
NCH = -(-E // CH)
EP = NCH * CH
NT = NCH * TPC
NB = -(-N // CH)
LAG = 3
TAIL_P = (N - (NB - 1) * CH) // TPC
R = 4
XR = 2 * R
PEEL = 2
LOAD_AHEAD = 2
STORE_LAG = 2 * R
FAR = 1 << 20
FMAX = 3.4028234663852886e38
EPS = 1e-5
SLOPE = 0.01
ZCOL = 1500
NZ = N * D // (P * ZCOL)
assert N * D % (P * ZCOL) == 0 and NZ == NCH + 1 and NB == 4 * NCH and NCH % R == 1


class Step:

    def __init__(self, q, a, b):
        self.q, self.a, self.b = q, a, b

    @property
    def at(self):
        return self.q * self.a + self.b

    def before(self, k):
        return Step(self.q, self.a, self.b - k)

    def slot(self, n):
        assert self.a % n == 0
        return self.b % n

    def turn(self, n):
        assert self.a % n == 0
        return self.q * (self.a // n) + self.b // n

    def is_block(self):
        return self.reached(0) and not (isinstance(self.q, int) and self.at >= NB)

    def reached(self, k):
        return self.a * (self.q if isinstance(self.q, int) else PEEL) + self.b >= k


def each_chunk(eng, step, after_first=None):
    for q in range(PEEL):
        for s in range(R):
            step(q, s)
        if q == 0 and after_first:
            after_first()
    with eng.Fori(PEEL, NCH // R) as q:
        for s in range(R):
            step(q, s)
    step(NCH // R, 0, last=True)


def chunk(q, s):
    return Step(q, R, s)


def block_a(q, s, t):
    return Step(q, 2 * R, 2 * s + t)


def block_s(q, s, t):
    return Step(q, 2 * R, 2 * NCH + 2 * s + t)


LAST_CHUNK = Step(NCH // R, R, 0)
LAST_BLOCK = Step(0, XR, NB - 1)
DRAIN = [LAST_BLOCK.before(-k) for k in range(1, 7)]


def gnn_kernel(nc, x, xt, src, dst, dst_next, dst_row, dst_prev, eat,
               w1m, w1e, w1r, b1, w2m, w2e, w2r, b2, out):
    f32 = mybir.dt.float32
    i32 = mybir.dt.int32
    ALU = mybir.AluOpType
    ACT = mybir.ActivationFunctionType
    ds = bass.ds

    table = nc.dram_tensor("agg1_table", (N, D), f32, kind="Internal").ap()
    mask_row = nc.dram_tensor("mask_row", (P, NT), f32, kind="Internal").ap()
    root_keep = nc.dram_tensor("root_keep", (NCH, D, CH), f32, kind="Internal").ap()
    c1d_keep = nc.dram_tensor("c1d_keep", (NCH, D, CH), f32, kind="Internal").ap()
    xd_keep = nc.dram_tensor("xd_keep", (NCH, P, TPC * D), f32, kind="Internal").ap()
    table_z = table.rearrange("n d -> (n d)").rearrange("(k p c) -> k p c", p=P, c=ZCOL)
    mask_c = mask_row.rearrange("p t -> (p t)").rearrange("(c o e) -> c o e", o=1, e=CH)
    out_b = out[0:(NB - 1) * CH, :].rearrange("(b p j) d -> b p (j d)", p=P, j=TPC)
    out_tail = out[(NB - 1) * CH:N, :].rearrange("(p j) d -> p (j d)", j=TPC)

    ctx = ExitStack()
    with ctx:
        def sb(name, shape, dt=f32):
            return ctx.enter_context(nc.sbuf_tensor(name, shape, dt))

        def pb(name, shape):
            return ctx.enter_context(nc.psum_tensor(name, shape, f32))

        def sem(name):
            return ctx.enter_context(nc.semaphore(name))

        def sems(name, n):
            return [sem(f"{name}{i}") for i in range(n)]

        ident = sb("ident", [P, P])
        wm1 = sb("wm1", [P, D])
        wm2 = sb("wm2", [P, D])
        wr1 = sb("wr1", [D + 1, D])
        wr2 = sb("wr2", [D + 1, D])
        b1c = sb("b1c", [D, 1])
        b2c = sb("b2c", [D, 1])
        epsc = sb("epsc", [P, 1])
        zero = sb("zero", [P, ZCOL])
        gat_i = sb("gat_i", [P, 2, NT], i32)
        dst_i = sb("dst_i", [P, NT], i32)
        dst_n = sb("dst_n", [P, NT], i32)
        end_i = sb("end_i", [P, NT], i32)
        eq_c = sb("eq_c", [P, NT])
        row_d = sb("row_d", [P, NT], i32)
        row_p = sb("row_p", [P, NT], i32)
        row_m = sb("row_m", [P, NT])
        now_gat = sb("now_gat", [P, R, 2, TPC], i32)
        now_end = sb("now_end", [P, R, TPC], i32)
        g_src = sb("g_src", [P, R, TPC * D])
        g_dst = sb("g_dst", [P, R, TPC * D])
        xe = sb("xe", [P, R, CH])
        mask = sb("mask", [D, R, CH])
        mx1 = sb("mx1", [D, 2, CH])
        rt1 = sb("rt1", [D, R, CH])
        mx2 = sb("mx2", [D, 2, CH])
        xd = sb("xd", [D, 2, CH])
        c1d = sb("c1d", [D, R, CH])
        yd = sb("yd", [D, 2, CH])
        yn = sb("yn", [P, 2, TPC * D])
        nat = sb("nat", [P, NT * D])
        stage = sb("stage", [P, 2, TPC * D])
        xtb = sb("xtb", [D + 1, XR, CH])
        c1t = sb("c1t", [D + 1, R, CH])
        c2t = sb("c2t", [D, R, CH])
        ob = sb("ob", [P, R, TPC * D])
        stat = sb("stat", [P, 4, TPC, 6])
        mv = sb("mv", [P, 4, TPC, 2])
        std = sb("std", [P, 4, TPC])
        rstd = sb("rstd", [P, 4, TPC])
        shift = sb("shift", [P, 2, TPC])
        idle = sb("idle", [1, 1])

        ps_t = pb("ps_t", [P, CH])
        ps_m = pb("ps_m", [P, CH])
        ps_r = pb("ps_r", [P, CH])
        ps_n = pb("ps_n", [P, CH])
        ps_1 = pb("ps_1", [P, CH])
        ps_2 = pb("ps_2", [P, CH])
        ps_y = [pb(f"ps_y{k}", [P, CH]) for k in range(2)]

        s_const = sem("s_const")
        s_index = sem("s_index")
        s_ident0 = sem("s_ident0")
        s_ident = sem("s_ident")
        s_epsc = sem("s_epsc")
        s_zero = sem("s_zero")
        s_ones = sem("s_ones")
        s_prep = sem("s_prep")
        s_mask_w = sem("s_mask_w")
        s_cleared = sem("s_cleared")
        l_src = sems("l_src", R)
        l_dst = sems("l_dst", R)
        l_ea = sems("l_ea", R)
        l_mask = sems("l_mask", R)
        l_xt = sems("l_xt", XR)
        l_rt = sems("l_rt", R)
        l_c1d = sems("l_c1d", R)
        l_xd = sems("l_xd", R)
        k_rt = sems("k_rt", R)
        k_c1d = sems("k_c1d", R)
        k_xd = sems("k_xd", R)
        o_st = sems("o_st", R)
        sc = sems("sc", 2)
        s_now = sem("s_now")
        s_end = sem("s_end")
        a_t = sem("a_t")
        a_xe = sem("a_xe")
        a_m = sem("a_m")
        a_scan = sem("a_scan")
        a_r = sem("a_r")
        a_rc = sem("a_rc")
        a_n = sem("a_n")
        a_nc = sem("a_nc")
        s_stage = sem("s_stage")
        a_own = sem("a_own")
        a_xd = sem("a_xd")
        a_r1 = sem("a_r1")
        a_z1 = sem("a_z1")
        a_c1 = sem("a_c1")
        b_t = sem("b_t")
        b_z1 = sem("b_z1")
        b_c1 = sem("b_c1")
        b_m = sem("b_m")
        b_scan = sem("b_scan")
        b_r = sem("b_r")
        b_z2 = sem("b_z2")
        b_n = sem("b_n")
        b_nc = sem("b_nc")
        e_c2 = sem("e_c2")
        e_y = sem("e_y")
        d_1 = sem("d_1")
        d_e1 = sem("d_e1")
        d_c1 = sem("d_c1")
        d_2 = sem("d_2")
        d_e2 = sem("d_e2")
        d_c2 = sem("d_c2")
        d_y = sem("d_y")
        d_n = sem("d_n")
        ln = [dict(stats=sem(f"ln_stats{k}"), mv=sem(f"ln_mv{k}"), std=sem(f"ln_std{k}"),
                   rstd=sem(f"ln_rstd{k}"), shift=sem(f"ln_shift{k}"), done=sem(f"ln_done{k}")) for k in "de"]
        DENSE, EDGE = 0, 1

        block = ctx.enter_context(nc.Block())

        def cols(j):
            return slice(j * P, (j + 1) * P)

        def row(j):
            return slice(j * D, (j + 1) * D)

        @block.gpsimd
        def _(pool):
            nc.gpsimd.memset(ident[:, :], 0.0).then_inc(s_ident0, 1)
            pool.wait_ge(s_ident0, 1)
            nc.gpsimd.affine_select(out=ident[:, :], in_=ident[:, :], compare_op=ALU.not_equal,
                                    fill=1.0, base=0, pattern=[[-1, P]],
                                    channel_multiplier=1).then_inc(s_ident, 1)

            def gather(rows, where, which, c, e, landed):
                for r in range(TPC):
                    nc.gpsimd.indirect_dma_start(
                        out=where[:, e.slot(R), row(r)], out_offset=None, in_=rows,
                        in_offset=bass.IndirectOffsetOnAxis(ap=now_gat[:, c.slot(R), which, r:r + 1], axis=0),
                    ).then_inc(landed[e.slot(R)], 16)

            def scatter(rows, e):
                for r in range(TPC):
                    nc.gpsimd.indirect_dma_start(
                        out=rows,
                        out_offset=bass.IndirectOffsetOnAxis(ap=now_end[:, e.slot(R), r:r + 1], axis=0),
                        in_=stage[:, e.slot(2), row(r)], in_offset=None, bounds_check=N - 1,
                        oob_is_err=False).then_inc(sc[e.slot(2)], 16)

            pool.wait_ge(s_index, 5 * 16)
            pool.wait_ge(s_prep, 6)

            def stage_gather(c):
                nc.gpsimd.tensor_copy(now_gat[:, c.slot(R), :, :], gat_i[:, :, ds(c.at * TPC, TPC)])\
                  .then_inc(s_now, 1)

            def stage_end(c, e):
                nc.gpsimd.tensor_copy(now_end[:, e.slot(R), :], end_i[:, ds(c.at * TPC, TPC)])\
                  .then_inc(s_end, 1)

            stage_gather(chunk(0, 0))

            def gather_a(q, s, last=False):
                c = chunk(q, s)
                if c.reached(R - 1):
                    f = c.before(R - 1)
                    pool.wait_ge(l_src[f.slot(R)], 64 * f.turn(R) + 64)
                    pool.wait_ge(l_dst[f.slot(R)], 64 * f.turn(R) + 64)
                if c.reached(R):
                    pool.wait_ge(a_t, c.before(R - 1).at)
                    pool.wait_ge(a_own, c.before(R - 1).at)
                    pool.wait_ge(k_xd[c.slot(R)], 16 * c.turn(R))
                pool.wait_ge(s_now, c.at + 1)
                if not last:
                    stage_gather(chunk(q, s + 1))
                gather(x, g_src, 0, c, c, l_src)
                gather(x, g_dst, 1, c, c, l_dst)

            each_chunk(pool, gather_a)
            pool.wait_ge(s_cleared, 16 * NZ)

            def scatter_step(rows, c, e, staged, last):
                if e.reached(R - 1):
                    f = e.before(R - 1)
                    pool.wait_ge(sc[f.slot(2)], 64 * f.turn(2) + 64)
                pool.wait_ge(staged, c.at + 1)
                pool.wait_ge(s_end, e.at + 1)
                if not last:
                    stage_end(c.before(-1), e.before(-1))
                scatter(rows, e)

            stage_end(chunk(0, 0), chunk(0, 0))
            each_chunk(pool, lambda q, s, last=False:
                       scatter_step(table, chunk(q, s), chunk(q, s), s_stage, last))
            for k in range(2):
                pool.wait_ge(sc[k], 64 * ((NCH + 1 - k) // 2))
            for k in range(R):
                pool.wait_ge(l_src[k], 64 * ((NCH + R - 1 - k) // R))
                pool.wait_ge(l_dst[k], 64 * ((NCH + R - 1 - k) // R))
            pool.wait_ge(a_t, NCH)
            stage_gather(chunk(0, 0))
            stage_end(chunk(0, 0), Step(0, R, NCH))

            def step_b(q, s, last=False):
                c = chunk(q, s)
                e = Step(q, R, NCH + s)
                if c.reached(R - 1):
                    f = e.before(R - 1)
                    pool.wait_ge(l_src[f.slot(R)], 64 * f.turn(R) + 64)
                if c.reached(R):
                    pool.wait_ge(b_t, c.before(R - 1).at)
                pool.wait_ge(s_now, e.at + 1)
                if not last:
                    stage_gather(chunk(q, s + 1))
                gather(table, g_src, 0, c, e, l_src)
                g = c.before(LAG)
                if g.reached(0):
                    if not g.reached(1):
                        for k in range(R):
                            pool.wait_ge(o_st[k], 16 * ((NB + R - 1 - k) // R))
                    scatter_step(out, g, e.before(LAG), ln[EDGE]["done"], False)

            each_chunk(pool, step_b)
            for i in range(LAG - 1, -1, -1):
                scatter_step(out, LAST_CHUNK.before(i), Step(0, R, 2 * NCH - 1 - i), ln[EDGE]["done"], i == 0)
            for k in range(2):
                pool.wait_ge(sc[k], 64 * ((2 * NCH + 1 - k) // 2))

        @block.sync
        def _(sp):
            sp.dma_start(gat_i[:, 0, :], src).then_inc(s_index, 16)
            sp.dma_start(dst_i[:, :], dst).then_inc(s_index, 16)
            sp.dma_start(dst_n[:, :], dst_next).then_inc(s_index, 16)
            sp.dma_start(row_d[:, :], dst_row).then_inc(s_index, 16)
            sp.dma_start(row_p[:, :], dst_prev).then_inc(s_index, 16)
            for to, of in ((wm1[0:D, :], w1m), (wm1[D:P, :], w1e), (wr1[0:D, :], w1r), (b1c[:, :], b1),
                           (wm2[0:D, :], w2m), (wm2[D:P, :], w2e), (wr2[0:D, :], w2r), (b2c[:, :], b2),
                           (wr1[D:D + 1, :], b1.rearrange("d o -> o d")),
                           (wr2[D:D + 1, :], b2.rearrange("d o -> o d"))):
                sp.dma_start(to, of).then_inc(s_const, 16)
            sp.wait_ge(s_prep, 6)
            sp.dma_start(mask_row, row_m[:, :]).then_inc(s_mask_w, 16)
            sp.wait_ge(s_mask_w, 16)

            def load_block(d):
                if not d.is_block():
                    return
                if d.reached(XR):
                    sp.wait_ge(d_y, d.before(XR - 1).at)
                sp.dma_start(xtb[0:D, d.slot(XR), :], xt[ds(d.at, 1), :, :].rearrange("o d e -> d (o e)"))\
                  .then_inc(l_xt[d.slot(XR)], 16)

            def store_block(d):
                if d.reached(0):
                    sp.wait_ge(ln[DENSE]["done"], d.at + 1)
                    sp.dma_start(out_b[ds(d.at, 1), :, :].rearrange("o p f -> p (o f)"),
                                 ob[:, d.slot(R), :]).then_inc(o_st[d.slot(R)], 16)

            def load_edges(c, e, used, scanned):
                k = e.slot(R)
                if c.reached(R):
                    sp.wait_ge(used, c.before(R - 1).at)
                    sp.wait_ge(scanned, c.before(R - 1).at)
                sp.dma_start(xe[D:P, k, :], eat[ds(c.at, 1), :, :].rearrange("o d e -> d (o e)"))\
                  .then_inc(l_ea[k], 16)
                sp.dma_start(mask[:, k, :],
                             mask_c[ds(c.at, 1), :, :].rearrange("c o e -> (c o) e").to_broadcast([D, CH]))\
                  .then_inc(l_mask[k], 16)

            def keep(where, c, what, ready, kept):
                if c.reached(0):
                    k = c.slot(R)
                    sp.wait_ge(ready, c.at + 1)
                    sp.dma_start(where[ds(c.at, 1), :, :].rearrange("o d e -> d (o e)"), what[:, k, :])\
                      .then_inc(kept[k], 16)

            def back(where, c, what, read, landed):
                k = c.slot(R)
                if c.reached(R):
                    sp.wait_ge(read, c.before(R - 1).at)
                sp.dma_start(what[:, k, :], where[ds(c.at, 1), :, :].rearrange("o d e -> d (o e)"))\
                  .then_inc(landed[k], 16)

            def keep_own(c):
                if c.reached(0):
                    k = c.slot(R)
                    sp.wait_ge(l_dst[k], 64 * c.turn(R) + 64)
                    sp.dma_start(xd_keep[ds(c.at, 1), :, :].rearrange("o d e -> d (o e)"), g_dst[:, k, :])\
                      .then_inc(k_xd[k], 16)

            def step_a(q, s, last=False):
                c, d0, d1 = chunk(q, s), block_a(q, s, 0), block_a(q, s, 1)
                if not last:
                    load_edges(c.before(-1), c.before(-1), a_r, a_scan)
                load_block(d0.before(-LOAD_AHEAD))
                keep_own(c.before(2))
                store_block(d0.before(STORE_LAG))
                keep(root_keep, c.before(3), rt1, a_rc, k_rt)
                load_block(d1.before(-LOAD_AHEAD))
                store_block(d1.before(STORE_LAG))
                keep(c1d_keep, c.before(3), c1d, a_c1, k_c1d)

            load_edges(chunk(0, 0), chunk(0, 0), a_r, a_scan)
            for i in range(LOAD_AHEAD):
                load_block(block_a(0, 0, i))
            each_chunk(sp, step_a)

            def keep_last():
                for i in range(2, -1, -1):
                    if i < 2:
                        keep_own(LAST_CHUNK.before(i))
                    keep(root_keep, LAST_CHUNK.before(i), rt1, a_rc, k_rt)
                    keep(c1d_keep, LAST_CHUNK.before(i), c1d, a_c1, k_c1d)

            def step_s(q, s, last=False):
                for t in range(2):
                    d = block_s(q, s, t)
                    load_block(d.before(-LOAD_AHEAD))
                    store_block(d.before(STORE_LAG))

            each_chunk(sp, step_s, after_first=keep_last)
            for k in range(R):
                for kept in (k_rt, k_c1d, k_xd):
                    sp.wait_ge(kept[k], 16 * ((NCH + R - 1 - k) // R))
            sp.wait_ge(a_r, NCH)
            sp.wait_ge(a_own, NCH)

            def step_b(q, s, last=False):
                c = chunk(q, s)
                back(root_keep, c, rt1, b_c1, l_rt)
                back(c1d_keep, c, c1d, b_r, l_c1d)
                load_edges(c, Step(q, R, NCH + s), b_m, b_scan)
                back(xd_keep, c, g_dst, e_y, l_xd)

            def store_last():
                for i in range(STORE_LAG - 1, 0, -1):
                    store_block(LAST_BLOCK.before(i))
                sp.wait_ge(ln[DENSE]["done"], NB)
                sp.dma_start(out_tail, ob[0:TAIL_P, LAST_BLOCK.slot(R), :])\
                  .then_inc(o_st[LAST_BLOCK.slot(R)], 16)

            each_chunk(sp, step_b, after_first=store_last)
            for k in range(R):
                sp.wait_ge(o_st[k], 16 * ((NB + R - 1 - k) // R))

        @block.tensor
        def _(pe):
            pe.wait_ge(s_ident, 1)
            pe.wait_ge(s_const, 10 * 16)
            pe.wait_ge(s_ones, 2)

            def forward(ps, rows, done):
                for r in range(TPC):
                    last = nc.tensor.transpose(ps[0:D, cols(r)], rows[:, row(r)], ident[:, :])
                last.then_inc(done, 1)

            def back(ps, t, done):
                for r in range(TPC):
                    last = nc.tensor.transpose(ps[:, row(r)], t[:, cols(r)], ident[0:D, 0:D])
                last.then_inc(done, 1)

            def product(ps, w, t, done):
                nc.tensor.matmul(ps[0:D, :], w, t, start=True, stop=True).then_inc(done, 1)

            def dense_1(d):
                if not d.is_block():
                    return
                pe.wait_ge(l_xt[d.slot(XR)], 16 * d.turn(XR) + 16)
                if d.reached(1):
                    pe.wait_ge(d_e1, d.at)
                product(ps_1, wr1[:, :], xtb[:, d.slot(XR), :], d_1)

            def dense_2(d):
                if not d.is_block():
                    return
                pe.wait_ge(d_c1, d.at + 1)
                if d.reached(1):
                    pe.wait_ge(d_e2, d.at)
                product(ps_2, wr2[:, :], c1t[:, d.slot(R), :], d_2)

            def dense_back(d):
                if d.is_block():
                    pe.wait_ge(d_y, d.at + 1)
                    if d.reached(2):
                        pe.wait_ge(ln[DENSE]["done"], d.before(1).at)
                    back(ps_y[d.slot(2)], c2t[:, d.slot(R), :], d_n)

            def dense(d):
                dense_1(d)
                dense_2(d.before(2))
                dense_back(d.before(4))

            def maxima_back(c):
                if c.reached(0):
                    pe.wait_ge(a_scan, c.at + 1)
                    if c.reached(1):
                        pe.wait_ge(a_nc, c.at)
                    back(ps_n, mx1[:, c.slot(2), :], a_n)

            def step_a(q, s, last=False):
                c, d0, d1 = chunk(q, s), block_a(q, s, 0), block_a(q, s, 1)
                k, u = c.slot(R), c.slot(2)
                pe.wait_ge(l_src[k], 64 * c.turn(R) + 64)
                if c.reached(1):
                    pe.wait_ge(a_xd, c.at)
                forward(ps_t, g_src[:, k, :], a_t)
                dense_1(d0)
                dense_2(d0.before(2))
                pe.wait_ge(l_dst[k], 64 * c.turn(R) + 64)
                pe.wait_ge(a_xe, c.at + 1)
                forward(ps_t, g_dst[:, k, :], a_own)
                maxima_back(c.before(1))
                dense_back(d0.before(4))
                pe.wait_ge(l_ea[k], 16 * c.turn(R) + 16)
                if c.reached(1):
                    pe.wait_ge(a_scan, c.at)
                product(ps_m, wm1[:, :], xe[:, k, :], a_m)
                if c.reached(1):
                    pe.wait_ge(a_z1, c.at)
                product(ps_r, wr1[0:D, :], xe[0:D, k, :], a_r)
                dense_1(d1)
                dense_2(d1.before(2))
                pe.wait_ge(a_xd, c.at + 1)
                pe.wait_ge(a_rc, c.at + 1)
                product(ps_r, wr1[0:D, :], xd[:, u, :], a_r1)
                dense_back(d1.before(4))

            each_chunk(pe, step_a)

            def step_s(q, s, last=False):
                for t in range(2):
                    dense(block_s(q, s, t))

            maxima_back(LAST_CHUNK)
            each_chunk(pe, step_s)
            for d in DRAIN:
                dense(d)
            pe.wait_ge(a_xd, NCH)
            pe.wait_ge(a_z1, NCH)
            pe.wait_ge(a_nc, NCH)

            def sums_back(c):
                if c.reached(0):
                    pe.wait_ge(b_z2, c.at + 1)
                    if c.reached(1):
                        pe.wait_ge(b_nc, c.at)
                    back(ps_n, yd[:, c.slot(2), :], b_n)

            def step_b(q, s, last=False):
                c, e = chunk(q, s), Step(q, R, NCH + s)
                k = c.slot(R)
                pe.wait_ge(l_src[e.slot(R)], 64 * e.turn(R) + 64)
                if c.reached(1):
                    pe.wait_ge(b_z1, c.at)
                forward(ps_t, g_src[:, e.slot(R), :], b_t)
                pe.wait_ge(l_c1d[k], 16 * c.turn(R) + 16)
                if c.reached(1):
                    pe.wait_ge(b_z2, c.at)
                product(ps_r, wr2[0:D, :], c1d[:, k, :], b_r)
                sums_back(c.before(1))
                pe.wait_ge(b_c1, c.at + 1)
                pe.wait_ge(l_ea[e.slot(R)], 16 * e.turn(R) + 16)
                if c.reached(1):
                    pe.wait_ge(b_scan, c.at)
                product(ps_m, wm2[:, :], xe[:, e.slot(R), :], b_m)

            each_chunk(pe, step_b)
            sums_back(LAST_CHUNK)

        @block.scalar
        def _(act):
            act.wait_ge(s_epsc, 1)
            act.wait_ge(s_zero, 1)

            def clear(i):
                act.dma_start(table_z[ds(i, 1), :, :].rearrange("o p c -> p (o c)"), zero[:, :])\
                   .then_inc(s_cleared, 16)

            def copy(to, of, done):
                nc.scalar.activation(to, of, ACT.Copy).then_inc(done, 1)

            def norm_std(kind, i):
                k = 2 * kind + i.slot(2)
                act.wait_ge(ln[kind]["mv"], i.at + 1)
                if i.reached(2):
                    act.wait_ge(ln[kind]["rstd"], i.before(1).at)
                nc.scalar.activation(std[:, k, :], mv[:, k, :, 1], ACT.Sqrt,
                                     bias=epsc[:, :]).then_inc(ln[kind]["std"], 1)

            def dense_std(d):
                if d.is_block():
                    norm_std(DENSE, d)

            def dense_e1(d):
                if not d.is_block():
                    return
                act.wait_ge(d_1, d.at + 1)
                if d.reached(R):
                    act.wait_ge(d_2, d.before(R - 1).at)
                copy(c1t[0:D, d.slot(R), :], ps_1[0:D, :], d_e1)

            def dense_e2(d):
                if not d.is_block():
                    return
                act.wait_ge(d_2, d.at + 1)
                if d.reached(R):
                    act.wait_ge(d_n, d.before(R - 1).at)
                copy(c2t[:, d.slot(R), :], ps_2[0:D, :], d_e2)

            def dense_norm(d):
                if d.is_block():
                    k = d.slot(2)
                    act.wait_ge(ln[DENSE]["shift"], d.at + 1)
                    if d.reached(R):
                        act.wait_ge(o_st[d.slot(R)], 16 * d.turn(R))
                    for r in range(TPC):
                        last = nc.scalar.activation(
                            ob[:, d.slot(R), row(r)], ps_y[k][:, row(r)], ACT.Identity,
                            bias=shift[:, k, r:r + 1], scale=rstd[:, k, r:r + 1])
                    last.then_inc(ln[DENSE]["done"], 1)

            def dense(d):
                dense_norm(d.before(6))
                dense_std(d.before(5))
                dense_e1(d)
                dense_e2(d.before(2))

            def maxima(c):
                if c.reached(0):
                    act.wait_ge(a_n, c.at + 1)
                    copy(nat[:, ds(c.at * TPC * D, TPC * D)], ps_n[:, 0:TPC * D], a_nc)

            def step_a(q, s, last=False):
                c, d0, d1 = chunk(q, s), block_a(q, s, 0), block_a(q, s, 1)
                k, u = c.slot(R), c.slot(2)
                dense_norm(d0.before(6))
                dense_std(d0.before(5))
                act.wait_ge(a_t, c.at + 1)
                if c.reached(R):
                    act.wait_ge(a_r, c.before(R - 1).at)
                copy(xe[0:D, k, :], ps_t[0:D, :], a_xe)
                clear(c.at)
                dense_e1(d0)
                dense_e2(d0.before(2))
                act.wait_ge(a_own, c.at + 1)
                if c.reached(2):
                    act.wait_ge(a_r1, c.before(1).at)
                copy(xd[:, u, :], ps_t[0:D, :], a_xd)
                maxima(c.before(1))
                dense_norm(d1.before(6))
                dense_std(d1.before(5))
                act.wait_ge(a_r, c.at + 1)
                if c.reached(R):
                    act.wait_ge(k_rt[k], 16 * c.turn(R))
                copy(rt1[:, k, :], ps_r[0:D, :], a_rc)
                dense_e1(d1)
                dense_e2(d1.before(2))

            clear(NZ - 1)
            each_chunk(act, step_a)
            maxima(LAST_CHUNK)

            def step_s(q, s, last=False):
                c = chunk(q, s)
                act.wait_ge(a_nc, c.at + 1)
                if c.reached(2):
                    act.wait_ge(sc[c.slot(2)], 64 * c.turn(2))
                copy(stage[:, c.slot(2), :], nat[:, ds(c.at * TPC * D, TPC * D)], s_stage)
                for t in range(2):
                    dense(block_s(q, s, t))

            each_chunk(act, step_s)
            for d in DRAIN:
                dense(d)

            def sums(c):
                if c.reached(0):
                    act.wait_ge(b_n, c.at + 1)
                    if c.reached(2):
                        act.wait_ge(ln[EDGE]["done"], c.before(1).at)
                    copy(yn[:, c.slot(2), :], ps_n[:, 0:TPC * D], b_nc)
                    norm_std(EDGE, c)

            each_chunk(act, lambda q, s, last=False: sums(chunk(q, s).before(1)))
            sums(LAST_CHUNK)
            act.wait_ge(s_cleared, 16 * NZ)

        @block.vector
        def _(dve):
            V = nc.vector
            V.memset(zero[:, :], 0.0).then_inc(s_zero, 1)
            V.memset(epsc[:, :], EPS).then_inc(s_epsc, 1)
            V.memset(xtb[D:D + 1, :, :], 1.0).then_inc(s_ones, 1)
            V.memset(c1t[D:D + 1, :, :], 1.0).then_inc(s_ones, 1)
            dve.wait_ge(s_index, 5 * 16)
            V.tensor_tensor(row_m[:, :], row_d[:, :], row_p[:, :], ALU.is_equal).then_inc(s_prep, 1)
            V.tensor_tensor(eq_c[:, :], dst_i[:, :], dst_n[:, :], ALU.is_equal).then_inc(s_prep, 1)
            dve.wait_ge(s_prep, 2)
            V.tensor_scalar(row_m[:, :], row_m[:, :], 2.0, -1.0, ALU.mult, ALU.add).then_inc(s_prep, 1)
            V.scalar_tensor_tensor(out=end_i[:, :], in0=eq_c[:, :], scalar=float(FAR), in1=dst_i[:, :],
                                   op0=ALU.mult, op1=ALU.add).then_inc(s_prep, 1)
            V.tensor_scalar(gat_i[:, 1, :], dst_i[:, :], float(N - 1), None, ALU.min).then_inc(s_prep, 1)
            dve.wait_ge(s_prep, 5)
            V.tensor_scalar(row_m[:, :], row_m[:, :], FMAX, None, ALU.mult).then_inc(s_prep, 1)
            dve.wait_ge(s_const, 10 * 16)

            def leaky(to, of, done):
                V.scalar_tensor_tensor(out=to, in0=of, scalar=SLOPE, in1=of,
                                       op0=ALU.mult, op1=ALU.max).then_inc(done, 1)

            def scan(c, mx, mk, done):
                if c.reached(1):
                    dve.wait_ge(done, c.at)
                    first = mx[:, c.before(1).slot(2), CH - 1:CH]
                else:
                    first = 0.0
                V.tensor_tensor_scan(mx[:, c.slot(2), :], mask[:, mk, :], ps_m[0:D, :], first,
                                     ALU.min, ALU.max).then_inc(done, 1)

            def dense_c1(d):
                if not d.is_block():
                    return
                dve.wait_ge(d_e1, d.at + 1)
                leaky(c1t[0:D, d.slot(R), :], c1t[0:D, d.slot(R), :], d_c1)

            def dense_c2(d):
                if not d.is_block():
                    return
                dve.wait_ge(d_e2, d.at + 1)
                leaky(c2t[:, d.slot(R), :], c2t[:, d.slot(R), :], d_c2)

            def dense_x(d):
                if not d.is_block():
                    return
                dve.wait_ge(d_c2, d.at + 1)
                dve.wait_ge(l_xt[d.slot(XR)], 16 * d.turn(XR) + 16)
                t = c2t[:, d.slot(R), :]
                V.tensor_tensor(t, t, xtb[0:D, d.slot(XR), :], ALU.add).then_inc(d_y, 1)

            def norm_stats(kind, i, rows):
                k = 2 * kind + i.slot(2)
                sm = ln[kind]
                if i.reached(2):
                    dve.wait_ge(sm["mv"], i.before(1).at)
                for r in range(TPC):
                    last = V.bn_stats(stat[:, k, r, :], rows(r))
                last.then_inc(sm["stats"], 1)

            def norm_aggr(kind, i):
                k = 2 * kind + i.slot(2)
                sm = ln[kind]
                dve.wait_ge(sm["stats"], i.at + 1)
                if i.reached(2):
                    dve.wait_ge(sm["done"], i.before(1).at)
                V.memset(idle[:, :], 0.0)
                for r in range(TPC):
                    last = V.bn_aggr(mv[:, k, r, :], stat[:, k, r, :])
                last.then_inc(sm["mv"], 1)

            def norm_rstd(kind, i):
                k = 2 * kind + i.slot(2)
                sm = ln[kind]
                dve.wait_ge(sm["std"], i.at + 1)
                if i.reached(2):
                    dve.wait_ge(sm["done"], i.before(1).at)
                V.reciprocal(rstd[:, k, :], std[:, k, :]).then_inc(sm["rstd"], 1)

            def dense_stats(d):
                if d.is_block():
                    dve.wait_ge(d_n, d.at + 1)
                    norm_stats(DENSE, d, lambda r: ps_y[d.slot(2)][:, row(r)])

            def dense_aggr(d):
                if d.is_block():
                    norm_aggr(DENSE, d)

            def dense_rstd(d):
                if d.is_block():
                    norm_rstd(DENSE, d)

            def dense_shift(d):
                if d.is_block():
                    k = d.slot(2)
                    dve.wait_ge(ln[DENSE]["rstd"], d.at + 1)
                    V.scalar_tensor_tensor(out=shift[:, k, :], in0=mv[:, k, :, 0], scalar=-1.0,
                                           in1=rstd[:, k, :], op0=ALU.mult, op1=ALU.mult)\
                     .then_inc(ln[DENSE]["shift"], 1)

            def dense_head(d):
                dense_c1(d.before(1))
                dense_c2(d.before(3))
                dense_rstd(d.before(5))

            def dense_tail(d):
                dense_x(d.before(3))
                dense_shift(d.before(5))
                dense_stats(d.before(4))
                dense_aggr(d.before(4))

            def step_a(q, s, last=False):
                c, d0, d1 = chunk(q, s), block_a(q, s, 0), block_a(q, s, 1)
                k, u = c.slot(R), c.slot(2)
                dense_head(d0)
                dense_tail(d0)
                dve.wait_ge(a_m, c.at + 1)
                dve.wait_ge(l_mask[k], 16 * c.turn(R) + 16)
                if c.reached(2):
                    dve.wait_ge(a_n, c.before(1).at)
                    dve.wait_ge(a_z1, c.before(1).at)
                scan(c, mx1, k, a_scan)
                dense_head(d1)
                dve.wait_ge(a_r1, c.at + 1)
                dve.wait_ge(a_scan, c.at + 1)
                if c.reached(R):
                    dve.wait_ge(k_c1d[k], 16 * c.turn(R))
                V.scalar_tensor_tensor(out=c1d[:, k, :], in0=ps_r[0:D, :], scalar=b1c[:, 0:1],
                                       in1=mx1[:, u, :], op0=ALU.add, op1=ALU.add).then_inc(a_z1, 1)
                dense_tail(d1)
                dve.wait_ge(a_z1, c.at + 1)
                leaky(c1d[:, k, :], c1d[:, k, :], a_c1)

            each_chunk(dve, step_a)

            def step_s(q, s, last=False):
                for t in range(2):
                    dense_head(block_s(q, s, t))
                    dense_tail(block_s(q, s, t))

            each_chunk(dve, step_s)
            for d in DRAIN:
                dense_head(d)
                dense_tail(d)

            def edge_aggr(c):
                if c.reached(0):
                    norm_aggr(EDGE, c)

            def edge_rstd(c):
                if c.reached(0):
                    norm_rstd(EDGE, c)

            def edge_norm(c):
                if c.reached(0):
                    e = Step(c.q, c.a, NCH + c.b)
                    dve.wait_ge(ln[EDGE]["rstd"], c.at + 1)
                    dve.wait_ge(sc[e.slot(2)], 64 * e.turn(2))
                    for r in range(TPC):
                        last = V.tensor_scalar(stage[:, e.slot(2), row(r)], yn[:, c.slot(2), row(r)],
                                               mv[:, 2 + c.slot(2), r, 0:1], rstd[:, 2 + c.slot(2), r:r + 1],
                                               ALU.subtract, ALU.mult)
                    last.then_inc(ln[EDGE]["done"], 1)

            def edge_c2(c):
                if c.reached(0):
                    dve.wait_ge(b_nc, c.at + 1)
                    leaky(yn[:, c.slot(2), :], yn[:, c.slot(2), :], e_c2)

            def edge_x(c):
                if c.reached(0):
                    dve.wait_ge(e_c2, c.at + 1)
                    dve.wait_ge(l_xd[c.slot(R)], 16 * c.turn(R) + 16)
                    t = yn[:, c.slot(2), :]
                    V.tensor_tensor(t, t, g_dst[:, c.slot(R), :], ALU.add).then_inc(e_y, 1)

            def edge_stats(c):
                if c.reached(0):
                    dve.wait_ge(e_y, c.at + 1)
                    norm_stats(EDGE, c, lambda r: yn[:, c.slot(2), row(r)])

            def step_b(q, s, last=False):
                c, e = chunk(q, s), Step(q, R, NCH + s)
                k, u = c.slot(R), c.slot(2)
                dve.wait_ge(b_t, c.at + 1)
                dve.wait_ge(l_rt[k], 16 * c.turn(R) + 16)
                V.scalar_tensor_tensor(out=rt1[:, k, :], in0=ps_t[0:D, :], scalar=b1c[:, 0:1],
                                       in1=rt1[:, k, :], op0=ALU.add, op1=ALU.add).then_inc(b_z1, 1)
                edge_rstd(c.before(2))
                dve.wait_ge(b_z1, c.at + 1)
                if c.reached(R):
                    dve.wait_ge(b_m, c.before(R - 1).at)
                leaky(xe[0:D, e.slot(R), :], rt1[:, k, :], b_c1)
                edge_norm(c.before(2))
                edge_c2(c.before(1))
                edge_x(c.before(1))
                dve.wait_ge(b_m, c.at + 1)
                dve.wait_ge(l_mask[e.slot(R)], 16 * e.turn(R) + 16)
                if c.reached(2):
                    dve.wait_ge(b_z2, c.before(1).at)
                scan(c, mx2, e.slot(R), b_scan)
                edge_stats(c.before(1))
                dve.wait_ge(b_r, c.at + 1)
                dve.wait_ge(b_scan, c.at + 1)
                if c.reached(2):
                    dve.wait_ge(b_n, c.before(1).at)
                V.scalar_tensor_tensor(out=yd[:, u, :], in0=ps_r[0:D, :], scalar=b2c[:, 0:1],
                                       in1=mx2[:, u, :], op0=ALU.add, op1=ALU.add).then_inc(b_z2, 1)
                edge_aggr(c.before(1))

            each_chunk(dve, step_b)
            edge_rstd(LAST_CHUNK.before(1))
            edge_norm(LAST_CHUNK.before(1))
            edge_c2(LAST_CHUNK)
            edge_x(LAST_CHUNK)
            edge_stats(LAST_CHUNK)
            norm_aggr(EDGE, LAST_CHUNK)
            edge_rstd(LAST_CHUNK)
            edge_norm(LAST_CHUNK)


def kernel(x, src, dst, edge_attr_32, L0_gnn_W1_msg, L0_gnn_W1_edge, L0_gnn_W1_root, L0_gnn_b1,
           L0_gnn_W2_msg, L0_gnn_W2_edge, L0_gnn_W2_root, L0_gnn_b2):
    import numpy as np
    import concourse.bacc as bacc
    from concourse.bass_utils import run_bass_kernel_spmd

    x = np.ascontiguousarray(x)
    src_p = np.zeros(EP, np.int32)
    src_p[:E] = src
    dst_p = np.full(EP + 2, FAR, np.int32)
    dst_p[0] = -1
    dst_p[1:E + 1] = dst
    xt = np.zeros((NB * CH, D), np.float32)
    xt[:N] = x
    xt = xt.reshape(NB, P, TPC, D).transpose(0, 3, 2, 1).reshape(NB, D, CH)
    ea = np.zeros((EP, DE), np.float32)
    ea[:E] = edge_attr_32
    column = lambda a: a.reshape(NT, P).T
    arrays = dict(
        x=x, xt=xt, src=column(src_p), dst=column(dst_p[1:EP + 1]), dst_next=column(dst_p[2:EP + 2]),
        dst_row=dst_p[1:EP + 1].reshape(P, NT), dst_prev=dst_p[0:EP].reshape(P, NT),
        eat=ea.reshape(NCH, CH, DE).transpose(0, 2, 1),
        w1m=L0_gnn_W1_msg, w1e=L0_gnn_W1_edge, w1r=L0_gnn_W1_root, b1=np.reshape(L0_gnn_b1, (D, 1)),
        w2m=L0_gnn_W2_msg, w2e=L0_gnn_W2_edge, w2r=L0_gnn_W2_root, b2=np.reshape(L0_gnn_b2, (D, 1)))
    nc = bacc.Bacc("TRN2", target_bir_lowering=False, num_devices=1)
    feed, args = {}, {}
    for name, a in arrays.items():
        a = np.ascontiguousarray(a)
        feed[f"in_{name}"] = a
        args[name] = nc.dram_tensor(f"in_{name}", a.shape, mybir.dt.from_np(a.dtype), kind="ExternalInput").ap()
    out = nc.dram_tensor("out_0", (N, D), mybir.dt.float32, kind="ExternalOutput").ap()
    gnn_kernel(nc, **args, out=out)
    return run_bass_kernel_spmd(nc, [feed], core_ids=[0]).results[0]["out_0"]
```
